# Optimizing a Trainium2 kernel written in Bass

```python
import numpy as np
import jax
import jax.numpy as jnp

def _softmax(x, axis=-1):
    return jax.nn.softmax(x, axis=axis)

def _gelu(x):
    return jax.nn.gelu(x, approximate=True)

def _silu(x):
    return jax.nn.silu(x)

def _sigmoid(x):
    return jax.nn.sigmoid(x)

def _layernorm(x, axis=-1, eps=1e-05):
    m = jnp.mean(x, axis=axis, keepdims=True)
    v = jnp.var(x, axis=axis, keepdims=True)
    return (x - m) / jnp.sqrt(v + eps)

def _scatter_add(tgt, idx, src, axis=0):
    return tgt.at[idx].add(src)

def _segment_sum(src, seg, n):
    return jax.ops.segment_sum(src, seg, n)
kernel_name = 'mk_adj_preln_d2_adj_r2_48e021'

def setup_inputs(seed: int=0):
    np.random.seed(seed)
    _w = jnp.asarray

    def _rec_inputs():
        import jax
        import jax.numpy as jnp
        _gk = jax.random.key(seed)
        x = -0.0001538 + 1 * jax.random.normal(jax.random.fold_in(_gk, 1), (16, 512, 384), jnp.float32)
        _a = jax.random.bernoulli(jax.random.fold_in(_gk, 2), 0.015625, (16, 512, 512))
        _a = jnp.logical_or(_a, jnp.swapaxes(_a, -1, -2))
        _a = jnp.logical_or(_a, jnp.eye(512, dtype=bool))
        adj = _a
        return (x, adj)
    x, adj = _rec_inputs()

    def _L0_gnn_setup():
        import jax, jax.numpy as jnp
        import numpy as np
        B, S, H = (4, 1024, 384)
        NUM_HEADS = 6
        HEAD_SIZE = H // NUM_HEADS
        NEG = -9000000000000000.0

        def _heads(x):
            b, s, _ = x.shape
            return x.reshape(b, s, NUM_HEADS, HEAD_SIZE).transpose(0, 2, 1, 3)
        key = jax.random.key(seed)
        ks = jax.random.split(key, 10)
        seq_inputs = jax.random.normal(ks[0], (B, S, H), dtype=jnp.float32)
        gm = jax.random.randint(ks[1], (B, S, S), 0, 2) > 0
        graph_mask = gm | jnp.eye(S, dtype=bool)[None]
        sc = 1.0 / np.sqrt(H)
        Wq = jax.random.normal(ks[2], (H, H), dtype=jnp.float32) * sc
        bq = jnp.zeros((H,), dtype=jnp.float32)
        Wk = jax.random.normal(ks[3], (H, H), dtype=jnp.float32) * sc
        bk = jnp.zeros((H,), dtype=jnp.float32)
        Wv = jax.random.normal(ks[4], (H, H), dtype=jnp.float32) * sc
        bv = jnp.zeros((H,), dtype=jnp.float32)
        Wf = jax.random.normal(ks[5], (H, H), dtype=jnp.float32) * sc
        bf = jnp.zeros((H,), dtype=jnp.float32)
        return {'seq_inputs': seq_inputs, 'Wq': Wq, 'bq': bq, 'Wk': Wk, 'bk': bk, 'Wv': Wv, 'bv': bv, 'Wf': Wf, 'bf': bf, 'graph_mask': graph_mask}
    _L0_gnn_all = _L0_gnn_setup()
    _L0_gnn_in = {k: v for k, v in _L0_gnn_all.items() if k in ('Wq', 'bq', 'Wk', 'bk', 'Wv', 'bv', 'Wf', 'bf')}
    del _L0_gnn_all

    def _L1_gnn_setup():
        import jax, jax.numpy as jnp
        import numpy as np
        ATT_HEAD = 12
        IN_DIM = 384
        OUT_DIM = IN_DIM // ATT_HEAD
        LEAKY_ALPHA = 0.2
        B, N = (8, 256)
        key = jax.random.key(seed)
        ks = jax.random.split(key, 8)
        feat_in = jax.random.normal(ks[0], (B, N, IN_DIM), dtype=jnp.float32)
        adj = jax.random.randint(ks[1], (B, N, N), 0, 2) > 0
        lim_W = float(np.sqrt(6.0 / (IN_DIM + OUT_DIM)))
        W = jax.random.uniform(ks[2], (ATT_HEAD, IN_DIM, OUT_DIM), minval=-lim_W, maxval=lim_W, dtype=jnp.float32)
        b = jnp.zeros((OUT_DIM,), dtype=jnp.float32)
        lim_w = float(np.sqrt(6.0 / (OUT_DIM + 1)))
        w_src = jax.random.uniform(ks[3], (ATT_HEAD, OUT_DIM, 1), minval=-lim_w, maxval=lim_w, dtype=jnp.float32)
        w_dst = jax.random.uniform(ks[4], (ATT_HEAD, OUT_DIM, 1), minval=-lim_w, maxval=lim_w, dtype=jnp.float32)
        std_H = float(np.sqrt(2.0 / (IN_DIM + IN_DIM)))
        H_w = jax.random.normal(ks[5], (IN_DIM, IN_DIM), dtype=jnp.float32) * std_H
        H_b = jax.random.normal(ks[6], (IN_DIM,), dtype=jnp.float32) * 0.01
        return {'feat_in': feat_in, 'adj': adj, 'W': W, 'b': b, 'w_src': w_src, 'w_dst': w_dst, 'H_w': H_w, 'H_b': H_b}
    _L1_gnn_all = _L1_gnn_setup()
    _L1_gnn_in = {k: v for k, v in _L1_gnn_all.items() if k in ('W', 'b', 'w_src', 'w_dst', 'H_w', 'H_b')}
    del _L1_gnn_all
    return {'x': x, 'adj': adj, 'L0_gnn_Wq': _L0_gnn_in['Wq'], 'L0_gnn_bq': _L0_gnn_in['bq'], 'L0_gnn_Wk': _L0_gnn_in['Wk'], 'L0_gnn_bk': _L0_gnn_in['bk'], 'L0_gnn_Wv': _L0_gnn_in['Wv'], 'L0_gnn_bv': _L0_gnn_in['bv'], 'L0_gnn_Wf': _L0_gnn_in['Wf'], 'L0_gnn_bf': _L0_gnn_in['bf'], 'L1_gnn_W': _L1_gnn_in['W'], 'L1_gnn_b': _L1_gnn_in['b'], 'L1_gnn_w_src': _L1_gnn_in['w_src'], 'L1_gnn_w_dst': _L1_gnn_in['w_dst'], 'L1_gnn_H_w': _L1_gnn_in['H_w'], 'L1_gnn_H_b': _L1_gnn_in['H_b']}

def reference(x, adj, L0_gnn_Wq, L0_gnn_bq, L0_gnn_Wk, L0_gnn_bk, L0_gnn_Wv, L0_gnn_bv, L0_gnn_Wf, L0_gnn_bf, L1_gnn_W, L1_gnn_b, L1_gnn_w_src, L1_gnn_w_dst, L1_gnn_H_w, L1_gnn_H_b):
    import jax
    import jax.numpy as jnp

    def _L0_gnn_ref(seq_inputs, Wq, bq, Wk, bk, Wv, bv, Wf, bf, graph_mask):
        import jax, jax.numpy as jnp
        import numpy as np
        B, S, H = (4, 1024, 384)
        NUM_HEADS = 6
        HEAD_SIZE = H // NUM_HEADS
        NEG = -9000000000000000.0

        def _heads(x):
            b, s, _ = x.shape
            return x.reshape(b, s, NUM_HEADS, HEAD_SIZE).transpose(0, 2, 1, 3)
        q = _heads(seq_inputs @ Wq + bq)
        k = _heads(seq_inputs @ Wk + bk)
        v = _heads(seq_inputs @ Wv + bv)
        scores = jnp.einsum('bhqd,bhkd->bhqk', q, k) / np.sqrt(HEAD_SIZE)
        bias = jnp.where(graph_mask, 0.0, NEG)[:, None]
        probs = jax.nn.softmax(scores + bias, axis=-1)
        ctx = jnp.einsum('bhqk,bhkd->bhqd', probs, v)
        ctx = ctx.transpose(0, 2, 1, 3).reshape(seq_inputs.shape[0], seq_inputs.shape[1], H)
        return ctx @ Wf + bf

    def _L1_gnn_ref(feat_in, adj, W, b, w_src, w_dst, H_w, H_b):
        import jax, jax.numpy as jnp
        import numpy as np
        ATT_HEAD = 12
        IN_DIM = 384
        OUT_DIM = IN_DIM // ATT_HEAD
        LEAKY_ALPHA = 0.2
        B, N = (8, 256)
        h = jnp.einsum('bnd,ade->bane', feat_in, W)
        th = jnp.tanh(h)
        attn_src = jnp.einsum('bane,aeo->bano', th, w_src)
        attn_dst = jnp.einsum('bane,aeo->bano', th, w_dst)
        attn = attn_src + jnp.swapaxes(attn_dst, 2, 3)
        attn = jnp.where(attn >= 0, attn, LEAKY_ALPHA * attn)
        mask = ~adj[:, None, :, :]
        attn = jnp.where(mask, jnp.float32(-999.0), attn)
        attn = jax.nn.softmax(attn, axis=-1)
        feat_out = jnp.einsum('banm,bame->bane', attn, h) + b
        feat_out = jnp.swapaxes(feat_out, 1, 2).reshape(feat_in.shape[0], feat_in.shape[1], -1)
        feat_out = jax.nn.elu(feat_out)
        gate = jax.nn.sigmoid(feat_in @ H_w.T + H_b)
        return gate * feat_out + (1.0 - gate) * feat_in
    h = jnp.maximum(_layernorm(x, axis=-1), 0.0)
    x = x + _L0_gnn_ref(h, L0_gnn_Wq, L0_gnn_bq, L0_gnn_Wk, L0_gnn_bk, L0_gnn_Wv, L0_gnn_bv, L0_gnn_Wf, L0_gnn_bf, adj)
    h = jnp.maximum(_layernorm(x, axis=-1), 0.0)
    x = x + _L1_gnn_ref(h, adj, L1_gnn_W, L1_gnn_b, L1_gnn_w_src, L1_gnn_w_dst, L1_gnn_H_w, L1_gnn_H_b)
    return x

_drawn_inputs = setup_inputs


def setup_inputs(seed=0):
    import zlib

    import numpy as np

    out = dict(_drawn_inputs(seed))
    spreads = {'L0_gnn_bq': (0.0, 0.8),
     'L0_gnn_bk': (0.0, 2.0),
     'L0_gnn_bv': (0.0, 0.1),
     'L0_gnn_bf': (0.0, 0.1),
     'L1_gnn_b': (0.0, 0.1)}
    factors = {'L1_gnn_w_src': 17.943, 'L1_gnn_H_b': 38.173}
    for name, (base, spread) in spreads.items():
        noise = np.random.default_rng([zlib.crc32(name.encode()), seed]).standard_normal(out[name].shape)
        drawn = base * np.exp(spread * noise) if base else spread * noise
        out[name] = jnp.asarray(drawn.astype(out[name].dtype))
    for name, factor in factors.items():
        out[name] = (out[name] * factor).astype(out[name].dtype)
    return out
```

```python
from contextlib import ExitStack

import numpy as np
import concourse.bass as bass
from concourse import mybir

F32 = mybir.dt.float32
F32R = mybir.dt.float32r
BF16 = mybir.dt.bfloat16
U8 = mybir.dt.uint8
ALU = mybir.AluOpType
ACT = mybir.ActivationFunctionType
AX_X = mybir.AxisListType.X

START = 1
B, N, D = 16, 512, 384
P = 128
TT = N // P
FC = D // P
NH0, DH0 = 6, 64
NPAIR = NH0 // 2
NH1, DH1 = 12, 32
HG = P // DH1
NG = NH1 // HG
EPS = 1e-5
NEG = 9000000000000000.0
SCALE = 1.0 / DH0 ** 0.5
LEAKY = 0.2
DROW = 32
ROWS = DROW + NH1

W_NORM1 = 0
W_ADJ = W_NORM1 + FC
W_QK = W_ADJ + TT
W_V = W_QK + 4
W_QK2 = W_V + TT
W_OUT = W_QK2 + 2
W_NORM2 = W_OUT + TT
W_FEAT = W_NORM2 + FC
W_TOK = W_FEAT + FC
W_ROWS = W_TOK + TT
W_GATE = W_ROWS + 1
W_FIN = W_GATE + TT
WORK = W_FIN + TT
assert WORK % 2 == 0


def qk_use(pair, which):
    return (W_QK + 2 * pair if pair < 2 else W_QK2) + which


def build(nc, x, adj, wq, wk, wv, wf, w1, hw, bqk, bv, bf, b1, hb, wsd, ident, sel, onehot, out):
    with ExitStack() as ctx:
        def sb(name, shape, dt=F32):
            return ctx.enter_context(nc.sbuf_tensor(name, shape, dt))

        def sem(name):
            return ctx.enter_context(nc.semaphore(name))

        names = ["wq", "wk", "wv", "wf", "w1", "hw"]
        w_dram = dict(zip(names, [wq, wk, wv, wf, w1, hw]))
        w_hi = {n: sb(n + "_hi", [P, FC, D], F32R) for n in names}
        w_lo = {n: sb(n + "_lo", [P, FC, D], F32R) for n in names}
        ident_f = sb("ident_f", [P, P])
        ident_b = sb("ident_b", [P, P], BF16)
        sel_r = sb("sel_r", [P, NH1, P], F32R)
        onehot_f = sb("onehot_f", [P, NG, DH1])
        bias_qk = sb("bias_qk", [P, 2 * NPAIR])
        bias_v, bias_f, bias_1, bias_h = (sb(n, [P, D]) for n in ("bias_v", "bias_f", "bias_1", "bias_h"))
        wsd_f = sb("wsd_f", [P, FC, ROWS])

        x_in = sb("x_in", [P, TT, D])
        adj_u8 = sb("adj_u8", [P, TT, N], U8)
        xres = sb("xres", [P, TT, D])
        hn = sb("hn", [P, TT, D])
        mask = sb("mask", [P, TT, N])
        adjT = sb("adjT", [P, TT, N], BF16)
        hT_hi = sb("hT_hi", [P, FC, N], F32R)
        hT_lo = sb("hT_lo", [P, FC, N], F32R)
        stats = sb("stats", [P, TT, 6])
        mv = sb("mv", [P, TT, 2])
        var = sb("var", [P, TT])
        rstd = sb("rstd", [P, TT])
        shift = sb("shift", [P, TT])
        mhalf = sb("mhalf", [P, TT])
        qs = sb("qs", [P, 2, 2, N], F32R)
        kh = sb("kh", [P, 2, 2, N], F32R)
        kl = sb("kl", [P, 2, 2, N], F32R)
        ctx_hi = sb("ctx_hi", [P, NPAIR, N], F32R)
        ctx_lo = sb("ctx_lo", [P, NPAIR, N], F32R)
        nmax = sb("nmax", [P, NH0, TT])
        rsum = sb("rsum", [P, NH0, TT])
        rinv = sb("rinv", [P, NH0, TT])
        r_rows = sb("r_rows", [P, N], F32R)
        uv_rows = sb("uv_rows", [ROWS, N])
        dstat = sb("dstat", [ROWS, 4])
        uvT = sb("uvT", [P, TT, ROWS])
        nvT = sb("nvT", [P, TT, ROWS])
        rden = sb("rden", [P, 2, NG, HG])

        KB = 256
        arena = sb("arena", [P, 49 * KB])

        def view(start_kb, *shape):
            n = int(np.prod(shape))
            v = arena[:, int(start_kb * KB):int(start_kb * KB) + n]
            if len(shape) == 1:
                return v
            names_ = "abc"[:len(shape)]
            return v.rearrange("p (%s) -> p %s" % (" ".join(names_), " ".join(names_)),
                               **{c: s for c, s in zip(names_, shape)})

        v_tok = view(0, TT, D)
        qk_f = view(6, 2, N)
        sm = view(10, 2, N)
        probs = view(14, 2 * TT, N)
        pT = view(30, 2 * TT, N)
        feat = view(0, FC, N)
        gate = view(0, TT, D)
        th = view(6, FC, N)
        numT = view(6, NG, N)
        h_tok = view(12, TT, D)
        t_ring = view(18, 4, N)
        edge = view(26, 8, N)
        denT = view(42, N)
        fin = view(44, 3, D)
        dd_rows = view(42, N)[0:ROWS]
        x_rows = view(44, N)[0:NH1]
        r_full = view(46, N)[0:NH1]
        adj_f = arena[:, 18 * KB:22 * KB].bitcast(BF16).rearrange("p (t n) -> p t n", t=TT)
        stage = [view(4.5 * i, FC, D) for i in range(6)]
        sel_stage = view(30, NH1, P)

        def bank(name):
            return ctx.enter_context(nc.psum_tensor(name, [P, N], F32))

        work = [bank("work0"), bank("work1")]
        score = [bank("score0"), bank("score1")]
        turn = [bank("turn0"), bank("turn1")]
        acc = [bank("acc0"), bank("acc1")]
        rbank = score + turn

        consts_in = sem("consts_in")
        split_hi = sem("split_hi")
        setup_done = sem("setup_done")
        pool_setup = sem("pool_setup")
        x_loaded = sem("x_loaded")
        adj_loaded = sem("adj_loaded")
        out_stored = sem("out_stored")
        stat_ready = sem("stat_ready")
        var_ready = sem("var_ready")
        rstd_ready = sem("rstd_ready")
        shift_ready = sem("shift_ready")
        hn_ready = sem("hn_ready")
        xb_ready = sem("xb_ready")
        mask_ready = sem("mask_ready")
        adjf_ready = sem("adjf_ready")
        work_full = sem("work_full")
        work_drained = [sem("work_drained0"), sem("work_drained1")]
        hi_ready = sem("hi_ready")
        qk_ready = sem("qk_ready")
        score_full = sem("score_full")
        smax_ready = sem("smax_ready")
        exp_ready = sem("exp_ready")
        rinv_ready = sem("rinv_ready")
        probs_ready = sem("probs_ready")
        turn_full = sem("turn_full")
        pT_ready = [sem("pT_ready0"), sem("pT_ready1")]
        ctx_full = sem("ctx_full")
        ctx_ready = sem("ctx_ready")
        x1_ready = sem("x1_ready")
        xh_ready = sem("xh_ready")
        gate_sum = sem("gate_sum")
        gate_ready = sem("gate_ready")
        dstat_step = sem("dstat_step")
        rows_ready = sem("rows_ready")
        rlo_ready = sem("rlo_ready")
        uv_full = sem("uv_full")
        uv_ready = sem("uv_ready")
        r_full_bank = sem("r_full_bank")
        t_ready = sem("t_ready")
        edge_ready = sem("edge_ready")
        agg_done = sem("agg_done")
        num_drained = sem("num_drained")
        fin_step = sem("fin_step")
        elu_exp = sem("elu_exp")
        out_ready = sem("out_ready")

        waits_passed = {e.engine: sem(f"waits_passed{i}")
                        for i, e in enumerate((nc.sync, nc.gpsimd, nc.vector, nc.tensor))}

        NCONST = 6 + 9

        def drained(eng, b, use):
            eng.wait_ge(work_drained[use % 2], START + b * (WORK // 2) + use // 2 + 1)

        def work_free(eng, b, use):
            eng.wait_ge(work_drained[use % 2], START + b * (WORK // 2) + use // 2)

        def prime(eng, *sems):
            for s in sems:
                eng.sem_inc(s, START)

        def settle(eng):
            eng.sem_inc(waits_passed[eng.engine], 1)

        def filled(eng, b, use):
            eng.wait_ge(work_full, b * WORK + use + 1)

        block = ctx.enter_context(nc.Block())

        @block.sync
        def _(sp):
            for n, s in zip(names, stage):
                sp.dma_start(s, w_dram[n].rearrange("(c p) n -> p c n", p=P)).then_inc(consts_in, 16)
            for dst, src in ((ident_f[:], ident), (sel_stage, sel.rearrange("p (h m) -> p h m", h=NH1)),
                             (onehot_f[:], onehot.rearrange("p (g m) -> p g m", g=NG)), (bias_qk[:], bqk),
                             (bias_v[:], bv), (bias_f[:], bf), (bias_1[:], b1), (bias_h[:], hb),
                             (wsd_f[:], wsd.rearrange("(c p) n -> p c n", p=P))):
                sp.dma_start(dst, src).then_inc(consts_in, 16)

            def load_x(b):
                sp.dma_start(x_in[:], x[b].rearrange("(t p) d -> p t d", p=P)).then_inc(x_loaded, 16)

            def load_adj(b):
                sp.dma_start(adj_u8[:], adj[b].rearrange("(t p) n -> p t n", p=P)).then_inc(adj_loaded, 16)

            def store(b):
                for t in range(TT):
                    sp.wait_ge(out_ready, b * TT + t + 1)
                    settle(sp)
                    sp.dma_start(out[b, t * P:(t + 1) * P, :], xres[:, t]).then_inc(out_stored, 16)

            load_x(0)
            load_adj(0)
            with sp.Fori(0, B - 1) as b:
                sp.wait_ge(xb_ready, b + 1)
                sp.wait_ge(hn_ready, b * 2 * TT + TT)
                settle(sp)
                load_x(b + 1)
                sp.wait_ge(mask_ready, b + 1)
                sp.wait_ge(adjf_ready, b + 1)
                settle(sp)
                load_adj(b + 1)
                store(b)
            store(B - 1)
            sp.wait_ge(out_stored, START + B * 16 * TT)

        @block.gpsimd
        def _(pool):
            prime(pool, out_stored)
            nc.gpsimd.memset(mhalf[:], -0.5).then_inc(pool_setup, 1)
            nc.gpsimd.memset(uv_rows[:], 0.0).then_inc(pool_setup, 1)
            pool.wait_ge(consts_in, 16 * NCONST)
            pool.wait_ge(pool_setup, 2)
            with pool.Fori(0, B) as b:
                pool.wait_ge(var_ready, 2 * b + 1)
                nc.gpsimd.tensor_tensor(rstd[:], var[:], mhalf[:], ALU.pow).then_inc(rstd_ready, 1)
                pool.wait_ge(x_loaded, 16 * b + 16)
                pool.wait_ge(out_stored, START + b * 16 * TT)
                for t in range(TT):
                    ins = nc.gpsimd.tensor_tensor(xres[:, t], x_in[:, t], bias_f[:], ALU.add)
                ins.then_inc(xb_ready, 1)
                pool.wait_ge(adj_loaded, 16 * b + 16)
                pool.wait_ge(smax_ready, START + b * NH0 * TT)
                settle(pool)
                for t in range(TT):
                    ins = nc.gpsimd.tensor_scalar(mask[:, t], adj_u8[:, t], -1.0, -NEG, ALU.add, ALU.mult)
                ins.then_inc(mask_ready, 1)
                for h in range(NH0):
                    pool.wait_ge(rinv_ready, START + b * NH0 + h + 1)
                    settle(pool)
                    for t in range(TT):
                        pr = probs[:, (h % 2) * TT + t]
                        nc.gpsimd.tensor_scalar(pr, pr, rinv[:, h, t:t + 1], 1.0,
                                                ALU.mult, ALU.mult).then_inc(probs_ready, 1)
                pool.wait_ge(var_ready, 2 * b + 2)
                nc.gpsimd.tensor_tensor(rstd[:], var[:], mhalf[:], ALU.pow).then_inc(rstd_ready, 1)
                for t in range(TT):
                    pool.wait_ge(hn_ready, b * 2 * TT + TT + t + 1)
                    nc.gpsimd.tensor_tensor(xres[:, t], xres[:, t], hn[:, t], ALU.add).then_inc(xh_ready, 1)

        @block.scalar
        def _(act):
            prime(act, t_ready, num_drained, pT_ready[1])
            act.wait_ge(consts_in, 16 * NCONST)
            for n, s in zip(names, stage):
                nc.scalar.activation(w_hi[n][:], s, ACT.Copy).then_inc(split_hi, 1)
            act.wait_ge(setup_done, 1)

            def norm(b, k, src):
                act.wait_ge(shift_ready, 2 * b + k + 1)
                if k == 0:
                    act.wait_ge(fin_step, START + b * 5 * TT)
                else:
                    filled(act, b, W_NORM1 + FC - 1)
                for t in range(TT):
                    nc.scalar.activation(hn[:, t], src[:, t], ACT.Relu, bias=shift[:, t:t + 1],
                                         scale=rstd[:, t:t + 1]).then_inc(hn_ready, 1)

            def turned_high(b, use):
                for c in range(FC):
                    filled(act, b, use + c)
                    nc.scalar.activation(hT_hi[:, c], work[(use + c) % 2][:], ACT.Copy).then_inc(hi_ready, 1)

            def qk_copy(b, p):
                s = p % 2
                for w, scale in ((0, -SCALE), (1, 1.0)):
                    use = qk_use(p, w)
                    ps = work[use % 2]
                    filled(act, b, use)
                    act.wait_ge(qk_ready, START + b * NPAIR + p)

                    def put(dst, lo, hi, bias_col=w * NPAIR + p):
                        return nc.scalar.activation(dst, ps[lo:hi], ACT.Identity, scale=scale,
                                                    bias=bias_qk[lo:hi, bias_col:bias_col + 1])
                    put(qk_f[:, w], 0, P)
                    for i in range(2):
                        lo, hi = i * DH0, (i + 1) * DH0
                        if w == 0:
                            last = put(qs[lo:hi, s, i], lo, hi)
                        else:
                            put(kh[0:DH0, s, i], lo, hi)
                            last = put(kh[DH0:P, s, i], lo, hi)
                    last.then_inc(work_drained[use % 2], 1)

            def exps(b, h):
                for t in range(TT):
                    i = h * TT + t
                    act.wait_ge(smax_ready, START + b * NH0 * TT + i + 1)
                    if t == 0:
                        if h >= 2:
                            act.wait_ge(turn_full, (b * NH0 + h - 1) * TT)
                        act.wait_ge(rinv_ready, START + b * NH0)
                    nc.scalar.activation(probs[:, (h % 2) * TT + t], sm[:, i % 2], ACT.Exp, scale=-1.0,
                                         bias=nmax[:, h, t:t + 1],
                                         accum_out=rsum[:, h, t:t + 1]).then_inc(exp_ready, 1)

            def pT_copy(b, h):
                if h >= 2:
                    act.wait_ge(ctx_full, b * NPAIR + h // 2)
                for c in (1, 3):
                    act.wait_ge(turn_full, (b * NH0 + h) * TT + c + 1)
                    nc.scalar.activation(pT[:, (h % 2) * TT + c], turn[1][:], ACT.Copy).then_inc(pT_ready[1], 1)

            def ctx_high(b, p):
                act.wait_ge(ctx_full, b * NPAIR + p + 1)
                nc.scalar.activation(ctx_hi[:, p], acc[p % 2][:], ACT.Copy).then_inc(hi_ready, 1)

            with act.Fori(0, B) as b:
                norm(b, 0, x_in)
                turned_high(b, W_NORM1)
                for c in range(TT):
                    use = W_ADJ + c
                    filled(act, b, use)
                    act.wait_ge(edge_ready, START + b * NH1 * TT)
                    nc.scalar.activation(adjT[:, c], work[use % 2][:, 0:N // 2].bitcast(BF16),
                                         ACT.Copy).then_inc(work_drained[use % 2], 1)
                qk_copy(b, 0)
                qk_copy(b, 1)
                exps(b, 0)
                exps(b, 1)
                qk_copy(b, 2)
                pT_copy(b, 0)
                exps(b, 2)
                pT_copy(b, 1)
                exps(b, 3)
                ctx_high(b, 0)
                pT_copy(b, 2)
                exps(b, 4)
                pT_copy(b, 3)
                exps(b, 5)
                ctx_high(b, 1)
                pT_copy(b, 4)
                pT_copy(b, 5)
                ctx_high(b, 2)

                norm(b, 1, xres)
                turned_high(b, W_NORM2)
                for c in range(FC):
                    use = W_FEAT + c
                    filled(act, b, use)
                    nc.scalar.activation(feat[:, c], work[use % 2][:], ACT.Copy)
                    nc.scalar.activation(th[:, c], work[use % 2][:], ACT.Tanh).then_inc(work_drained[use % 2], 1)
                drained(act, b, W_ROWS)
                nc.scalar.activation(uv_rows[0:NH1], dd_rows[DROW:ROWS], ACT.Exp)
                nc.scalar.activation(uv_rows[DROW:ROWS], dd_rows[DROW:ROWS], ACT.Exp,
                                     scale=LEAKY).then_inc(rows_ready, 1)
                nc.scalar.activation(r_full, x_rows, ACT.Exp, scale=1.0 - LEAKY)
                nc.scalar.activation(r_rows[0:NH1], x_rows, ACT.Exp, scale=1.0 - LEAKY).then_inc(rows_ready, 1)
                for t in range(TT):
                    drained(act, b, W_GATE + t)
                    nc.scalar.activation(gate[:, t], gate[:, t], ACT.Tanh, scale=0.5).then_inc(gate_ready, 1)
                act.wait_ge(uv_ready, 2 * b + 2)
                for g in range(NG):
                    for c in range(TT):
                        for j in range(HG):
                            k = (g * TT + c) * HG + j
                            if c == 0:
                                act.wait_ge(r_full_bank, b * NH1 + g * HG + j + 1)
                            if k >= 4:
                                act.wait_ge(edge_ready, START + b * NH1 * TT + k - 3)
                            a = g * HG + j
                            nc.scalar.activation(t_ring[:, k % 4], rbank[j][:], ACT.Relu, scale=uvT[:, c, a:a + 1],
                                                 bias=nvT[:, c, DROW + a:DROW + a + 1]).then_inc(t_ready, 1)
                    act.wait_ge(agg_done, b * NG * TT + (g + 1) * TT)
                    nc.scalar.activation(numT[:, g], acc[0][:], ACT.Copy).then_inc(num_drained, 1)
                nc.scalar.activation(denT, acc[1][:], ACT.Copy).then_inc(num_drained, 1)
                for t in range(TT):
                    act.wait_ge(fin_step, START + b * 5 * TT + 5 * t + 2)
                    nc.scalar.activation(fin[:, 1], fin[:, 1], ACT.Exp).then_inc(elu_exp, 1)

        @block.vector
        def _(dve):
            prime(dve, smax_ready, fin_step, edge_ready, qk_ready, rinv_ready, pT_ready[0], *work_drained)
            nc.vector.memset(r_rows[:].bitcast(F32), 0.0)
            dve.wait_ge(consts_in, 16 * NCONST)
            nc.vector.tensor_copy(ident_b[:], ident_f[:])
            nc.vector.tensor_copy(sel_r[:], sel_stage)
            nc.vector.tensor_scalar(bias_qk[:, 0:NPAIR], bias_qk[:, 0:NPAIR], -SCALE, None, ALU.mult)
            for i, (n, s) in enumerate(zip(names, stage)):
                dve.wait_ge(split_hi, i + 1)
                ins = nc.vector.tensor_tensor(w_lo[n][:], s, w_hi[n][:].bitcast(F32), ALU.subtract)
            ins.then_inc(setup_done, 1)

            def tile_stats(b, k, t, src):
                n0 = (2 * b + k) * 2 * TT + 2 * t
                nc.vector.bn_stats(stats[:, t], src[:, t]).then_inc(stat_ready, 1)
                dve.wait_ge(stat_ready, n0 + 1)
                settle(dve)
                nc.vector.bn_aggr(mv[:, t], stats[:, t]).then_inc(stat_ready, 1)

            def norm_rest(b, k):
                dve.wait_ge(stat_ready, (2 * b + k + 1) * 2 * TT)
                nc.vector.tensor_scalar(var[:], mv[:, :, 1], EPS, None, ALU.add).then_inc(var_ready, 1)
                dve.wait_ge(rstd_ready, 2 * b + k + 1)
                nc.vector.scalar_tensor_tensor(out=shift[:], in0=mv[:, :, 0], scalar=-1.0, in1=rstd[:],
                                               op0=ALU.mult, op1=ALU.mult).then_inc(shift_ready, 1)

            def turned_low(b, use, first):
                for c in range(FC):
                    dve.wait_ge(hi_ready, b * (2 * FC + NPAIR) + first + c + 1)
                    u = use + c
                    nc.vector.tensor_tensor(hT_lo[:, c], work[u % 2][:], hT_hi[:, c].bitcast(F32),
                                            ALU.subtract).then_inc(work_drained[u % 2], 1)

            def qk_low(b, p):
                s = p % 2
                drained(dve, b, qk_use(p, 0))
                for i in range(2):
                    lo, hi = i * DH0, (i + 1) * DH0
                    o = (1 - i) * DH0
                    nc.vector.tensor_tensor(qs[o:o + DH0, s, i], qk_f[lo:hi, 0], qs[lo:hi, s, i].bitcast(F32),
                                            ALU.subtract)
                drained(dve, b, qk_use(p, 1))
                for i in range(2):
                    lo, hi = i * DH0, (i + 1) * DH0
                    for o in (0, DH0):
                        ins = nc.vector.tensor_tensor(kl[o:o + DH0, s, i], qk_f[lo:hi, 1],
                                                      kh[lo:hi, s, i].bitcast(F32), ALU.subtract)
                ins.then_inc(qk_ready, 1)

            def maxima(b, h, tiles):
                for t in tiles:
                    i = h * TT + t
                    dve.wait_ge(score_full, b * NH0 * TT + i + 1)
                    if i >= 2:
                        dve.wait_ge(exp_ready, b * NH0 * TT + i - 1)
                    settle(dve)
                    nc.vector.tensor_tensor_reduce(sm[:, i % 2], score[i % 2][:], mask[:, t], 1.0, 3.0e38,
                                                   ALU.add, ALU.min, nmax[:, h, t:t + 1]).then_inc(smax_ready, 1)

            def inverse(b, h):
                dve.wait_ge(exp_ready, (b * NH0 + h + 1) * TT)
                nc.vector.reciprocal(rinv[:, h], rsum[:, h]).then_inc(rinv_ready, 1)

            def pT_copy(b, h):
                if h >= 2:
                    dve.wait_ge(ctx_full, b * NPAIR + h // 2)
                for c in (0, 2):
                    dve.wait_ge(turn_full, (b * NH0 + h) * TT + c + 1)
                    nc.vector.tensor_copy(pT[:, (h % 2) * TT + c], turn[0][:]).then_inc(pT_ready[0], 1)

            def ctx_low(b, p):
                dve.wait_ge(hi_ready, b * (2 * FC + NPAIR) + FC + p + 1)
                nc.vector.tensor_tensor(ctx_lo[:, p], acc[p % 2][:], ctx_hi[:, p].bitcast(F32),
                                        ALU.subtract).then_inc(ctx_ready, 1)

            with dve.Fori(0, B) as b:
                dve.wait_ge(x_loaded, 16 * b + 16)
                for t in range(TT):
                    tile_stats(b, 0, t, x_in)
                norm_rest(b, 0)
                dve.wait_ge(adj_loaded, 16 * b + 16)
                nc.vector.tensor_copy(adj_f, adj_u8[:]).then_inc(adjf_ready, 1)
                turned_low(b, W_NORM1, 0)
                qk_low(b, 0)
                qk_low(b, 1)
                for t in range(TT):
                    use = W_V + t
                    filled(dve, b, use)
                    nc.vector.tensor_tensor(v_tok[:, t], work[use % 2][:, 0:D], bias_v[:],
                                            ALU.add).then_inc(work_drained[use % 2], 1)
                dve.wait_ge(mask_ready, b + 1)
                maxima(b, 0, range(TT))
                maxima(b, 1, [0])
                inverse(b, 0)
                maxima(b, 1, range(1, TT))
                qk_low(b, 2)
                pT_copy(b, 0)
                maxima(b, 2, [0])
                inverse(b, 1)
                maxima(b, 2, range(1, TT))
                pT_copy(b, 1)
                maxima(b, 3, [0])
                inverse(b, 2)
                maxima(b, 3, range(1, TT))
                ctx_low(b, 0)
                pT_copy(b, 2)
                maxima(b, 4, [0])
                inverse(b, 3)
                maxima(b, 4, range(1, TT))
                pT_copy(b, 3)
                maxima(b, 5, [0])
                inverse(b, 4)
                maxima(b, 5, range(1, TT))
                inverse(b, 5)
                ctx_low(b, 1)
                pT_copy(b, 4)
                pT_copy(b, 5)
                ctx_low(b, 2)

                dve.wait_ge(xb_ready, b + 1)
                for t in range(TT):
                    use = W_OUT + t
                    filled(dve, b, use)
                    nc.vector.tensor_tensor(xres[:, t], work[use % 2][:, 0:D], xres[:, t],
                                            ALU.add).then_inc(work_drained[use % 2], 1)
                    drained(dve, b, use)
                    tile_stats(b, 1, t, xres)
                norm_rest(b, 1)
                turned_low(b, W_NORM2, FC + NPAIR)
                for t in range(TT):
                    use = W_TOK + t
                    filled(dve, b, use)
                    nc.vector.tensor_tensor(h_tok[:, t], work[use % 2][:, 0:D], bias_1[:],
                                            ALU.add).then_inc(work_drained[use % 2], 1)
                s0 = b * 5
                filled(dve, b, W_ROWS)
                rows = work[W_ROWS % 2]
                nc.vector.tensor_reduce(dstat[DROW:ROWS, 0:1], rows[DROW:ROWS], AX_X, ALU.max).then_inc(dstat_step, 1)
                nc.vector.tensor_reduce(dstat[DROW:ROWS, 1:2], rows[DROW:ROWS], AX_X, ALU.min).then_inc(dstat_step, 1)
                dve.wait_ge(dstat_step, s0 + 2)
                nc.vector.tensor_tensor(dstat[DROW:ROWS, 1:2], dstat[DROW:ROWS, 0:1], dstat[DROW:ROWS, 1:2],
                                        ALU.subtract).then_inc(dstat_step, 1)
                dve.wait_ge(dstat_step, s0 + 3)
                nc.vector.tensor_copy(dstat[0:NH1, 0:2], dstat[DROW:ROWS, 0:2]).then_inc(dstat_step, 1)
                nc.vector.tensor_scalar(dd_rows[DROW:ROWS], rows[DROW:ROWS], dstat[DROW:ROWS, 0:1], None,
                                        ALU.subtract).then_inc(dstat_step, 1)
                dve.wait_ge(dstat_step, s0 + 5)
                nc.vector.tensor_scalar(x_rows, rows[0:NH1], dstat[0:NH1, 0:1], dstat[0:NH1, 1:2],
                                        ALU.add, ALU.min).then_inc(work_drained[W_ROWS % 2], 1)
                for t in range(TT):
                    use = W_GATE + t
                    filled(dve, b, use)
                    nc.vector.tensor_tensor(gate[:, t], work[use % 2][:, 0:D], bias_h[:],
                                            ALU.add).then_inc(work_drained[use % 2], 1)
                    if t == 0:
                        dve.wait_ge(rows_ready, 2 * b + 2)
                        nc.vector.tensor_tensor(r_rows[DROW:ROWS], r_full, r_rows[0:NH1].bitcast(F32),
                                                ALU.subtract).then_inc(rlo_ready, 1)
                dve.wait_ge(uv_full, b + 1)
                uv_ps = score[0][:, 0:TT * ROWS].rearrange("p (c r) -> p c r", c=TT)
                nc.vector.tensor_copy(uvT[:], uv_ps).then_inc(uv_ready, 1)
                nc.vector.tensor_scalar(nvT[:], uv_ps, -1.0, None, ALU.mult).then_inc(uv_ready, 1)
                dve.wait_ge(uv_ready, 2 * b + 2)
                for g in range(NG):
                    for c in range(TT):
                        for j in range(HG):
                            k = (g * TT + c) * HG + j
                            dve.wait_ge(t_ready, START + b * NH1 * TT + k + 1)
                            if j == 0 and g * TT + c >= 2:
                                dve.wait_ge(agg_done, b * NG * TT + g * TT + c - 1)
                            a = DROW + g * HG + j
                            nc.vector.scalar_tensor_tensor(out=edge[:, k % 8], in0=t_ring[:, k % 4],
                                                           scalar=uvT[:, c, a:a + 1], in1=adjT[:, c],
                                                           op0=ALU.add, op1=ALU.mult).then_inc(edge_ready, 1)
                dve.wait_ge(gate_ready, (b + 1) * TT)
                dve.wait_ge(xh_ready, (b + 1) * TT)
                for t in range(TT):
                    n0 = b * 5 * TT + 5 * t
                    use = W_FIN + t
                    ps = work[use % 2]
                    filled(dve, b, use)
                    nc.vector.reciprocal(rden[:, t % 2], ps[:, D:N].rearrange("p (j s) -> p s j", j=HG)[:, 0:NG]
                                         ).then_inc(fin_step, 1)
                    dve.wait_ge(fin_step, START + n0 + 1)
                    nc.vector.tensor_tensor(fin[:, 0].rearrange("p (a e) -> p a e", a=NH1),
                                            ps[:, 0:D].rearrange("p (a e) -> p a e", a=NH1),
                                            rden[:, t % 2].rearrange("p g j -> p (g j)").unsqueeze(2)
                                            .to_broadcast([P, NH1, DH1]), ALU.mult).then_inc(work_drained[use % 2], 1)
                    drained(dve, b, use)
                    nc.vector.tensor_scalar(fin[:, 1], fin[:, 0], 0.0, None, ALU.min).then_inc(fin_step, 1)
                    dve.wait_ge(elu_exp, b * TT + t + 1)
                    nc.vector.scalar_tensor_tensor(out=fin[:, 2], in0=fin[:, 0], scalar=0.0, in1=fin[:, 1],
                                                   op0=ALU.max, op1=ALU.add).then_inc(fin_step, 1)
                    dve.wait_ge(fin_step, START + n0 + 3)
                    nc.vector.scalar_tensor_tensor(out=fin[:, 0], in0=fin[:, 2], scalar=-1.0, in1=hn[:, t],
                                                   op0=ALU.add, op1=ALU.subtract).then_inc(fin_step, 1)
                    dve.wait_ge(fin_step, START + n0 + 4)
                    nc.vector.scalar_tensor_tensor(out=fin[:, 2], in0=gate[:, t], scalar=1.0, in1=fin[:, 0],
                                                   op0=ALU.add, op1=ALU.mult).then_inc(fin_step, 1)
                    dve.wait_ge(fin_step, START + n0 + 5)
                    nc.vector.scalar_tensor_tensor(out=xres[:, t], in0=fin[:, 2], scalar=0.5, in1=xres[:, t],
                                                   op0=ALU.mult, op1=ALU.add).then_inc(out_ready, 1)

        @block.tensor
        def _(pe):
            pe.wait_ge(setup_done, 1)

            def three(ps, l_hi, l_lo, r_hi, r_lo):
                n = 0
                for c in range(FC):
                    for l, r in ((l_hi, r_hi), (l_hi, r_lo), (l_lo, r_hi)):
                        ins = nc.tensor.matmul(ps, l(c), r(c), start=(n == 0), stop=(n == 3 * FC - 1))
                        n += 1
                return ins

            def cols(t, lo, hi=None):
                return lambda c: t[:, c, lo:lo + P]

            def whole(t):
                return lambda c: t[:, c, :]

            def turn_norm(b, k, use):
                for c in range(FC):
                    u = use + c
                    work_free(pe, b, u)
                    for t in range(TT):
                        if c == 0:
                            pe.wait_ge(hn_ready, (2 * b + k) * TT + t + 1)
                        ins = nc.tensor.transpose(work[u % 2][:, t * P:(t + 1) * P], hn[:, t, c * P:(c + 1) * P],
                                                  ident_f[:])
                    ins.then_inc(work_full, 1)

            def by_feature(b, use, w, c):
                work_free(pe, b, use)
                three(work[use % 2][:], cols(w_hi[w], c * P), cols(w_lo[w], c * P), whole(hT_hi),
                      whole(hT_lo)).then_inc(work_full, 1)

            def by_node(b, use, l_hi, l_lo, w, t):
                work_free(pe, b, use)
                three(work[use % 2][:, 0:D], cols(l_hi, t * P), cols(l_lo, t * P), whole(w_hi[w]),
                      whole(w_lo[w])).then_inc(work_full, 1)

            def scores(b, h):
                s, i = (h // 2) % 2, h % 2
                if i == 0:
                    pe.wait_ge(qk_ready, START + b * NPAIR + h // 2 + 1)
                for t in range(TT):
                    n = h * TT + t
                    if n < 2:
                        pe.wait_ge(t_ready, START + b * NH1 * TT)
                    else:
                        pe.wait_ge(smax_ready, START + b * NH0 * TT + n - 1)
                    q = qs[:, s, i, t * P:(t + 1) * P]
                    nc.tensor.matmul(score[n % 2][:], q, kh[:, s, i], start=True, stop=False)
                    nc.tensor.matmul(score[n % 2][:], q, kl[:, s, i], start=False, stop=True).then_inc(score_full, 1)

            def turn_probs(b, h):
                for c in range(TT):
                    n = h * TT + c
                    for t in range(TT):
                        if c == 0:
                            pe.wait_ge(probs_ready, b * NH0 * TT + h * TT + t + 1)
                        if t == 0:
                            pe.wait_ge(pT_ready[c % 2], START + b * NH0 * 2 + n // 2)
                        ins = nc.tensor.transpose(turn[c % 2][:, t * P:(t + 1) * P],
                                                  probs[:, (h % 2) * TT + t, c * P:(c + 1) * P], ident_f[:])
                    ins.then_inc(turn_full, 1)

            def context(b, p):
                if p == 0:
                    pe.wait_ge(num_drained, START + b * (NG + 1))
                if p == 2:
                    pe.wait_ge(ctx_ready, b * NPAIR + 1)
                for c in range(TT):
                    pe.wait_ge(pT_ready[c % 2], START + b * NH0 * 2 + (2 * p + 1) * 2 + c // 2 + 1)
                    for i in range(2):
                        f = (2 * p + i) * DH0
                        ins = nc.tensor.matmul(acc[p % 2][i * DH0:(i + 1) * DH0], v_tok[:, c, f:f + DH0],
                                               pT[:, i * TT + c], start=(c == 0), stop=(c == TT - 1))
                ins.then_inc(ctx_full, 1)

            with pe.Fori(0, B) as b:
                turn_norm(b, 0, W_NORM1)
                pe.wait_ge(adjf_ready, b + 1)
                for c in range(TT):
                    u = W_ADJ + c
                    work_free(pe, b, u)
                    for t in range(TT):
                        ins = nc.tensor.transpose(work[u % 2][:, t * P // 2:(t + 1) * P // 2].bitcast(BF16),
                                                  adj_f[:, t, c * P:(c + 1) * P], ident_b[:])
                    ins.then_inc(work_full, 1)
                drained(pe, b, W_NORM1 + 1)
                drained(pe, b, W_NORM1 + 2)
                for p in range(2):
                    by_feature(b, qk_use(p, 0), "wq", p)
                    by_feature(b, qk_use(p, 1), "wk", p)
                for t in range(TT):
                    by_node(b, W_V + t, hT_hi, hT_lo, "wv", t)
                scores(b, 0)
                scores(b, 1)
                by_feature(b, qk_use(2, 0), "wq", 2)
                by_feature(b, qk_use(2, 1), "wk", 2)
                drained(pe, b, W_V + TT - 1)
                turn_probs(b, 0)
                scores(b, 2)
                turn_probs(b, 1)
                scores(b, 3)
                context(b, 0)
                turn_probs(b, 2)
                scores(b, 4)
                turn_probs(b, 3)
                scores(b, 5)
                context(b, 1)
                turn_probs(b, 4)
                turn_probs(b, 5)
                context(b, 2)
                pe.wait_ge(ctx_ready, (b + 1) * NPAIR)
                for t in range(TT):
                    by_node(b, W_OUT + t, ctx_hi, ctx_lo, "wf", t)

                turn_norm(b, 1, W_NORM2)
                drained(pe, b, W_NORM2 + 1)
                drained(pe, b, W_NORM2 + 2)
                for c in range(FC):
                    by_feature(b, W_FEAT + c, "w1", c)
                drained(pe, b, W_FEAT + 1)
                drained(pe, b, W_FEAT + 2)
                for t in range(TT):
                    u = W_TOK + t
                    work_free(pe, b, u)
                    for c in range(FC):
                        ins = nc.tensor.transpose(work[u % 2][:, c * P:(c + 1) * P], feat[:, c, t * P:(t + 1) * P],
                                                  ident_f[:])
                    ins.then_inc(work_full, 1)
                work_free(pe, b, W_ROWS)
                for c in range(FC):
                    ins = nc.tensor.matmul(work[W_ROWS % 2][0:ROWS], wsd_f[:, c], th[:, c], start=(c == 0),
                                           stop=(c == FC - 1))
                ins.then_inc(work_full, 1)
                for t in range(TT):
                    by_node(b, W_GATE + t, hT_hi, hT_lo, "hw", t)
                pe.wait_ge(rows_ready, 2 * b + 1)
                settle(pe)
                for c in range(TT):
                    ins = nc.tensor.transpose(score[0][:, c * ROWS:(c + 1) * ROWS], uv_rows[:, c * P:(c + 1) * P],
                                              ident_f[0:ROWS, 0:ROWS])
                ins.then_inc(uv_full, 1)
                pe.wait_ge(rlo_ready, b + 1)
                pe.wait_ge(uv_ready, 2 * b + 2)

                def spread(g, j):
                    if g > 0:
                        pe.wait_ge(t_ready, START + b * NH1 * TT + ((g - 1) * TT + TT - 1) * HG + j + 1)
                    nc.tensor.matmul(rbank[j][:], sel_r[:, g * HG + j], r_rows[:], start=True,
                                     stop=True).then_inc(r_full_bank, 1)

                drained(pe, b, W_TOK + TT - 1)
                drained(pe, b, W_TOK + TT - 2)
                for j in range(HG):
                    spread(0, j)
                for g in range(NG):
                    for c in range(TT):
                        n = g * TT + c
                        pe.wait_ge(edge_ready, START + b * NH1 * TT + (n + 1) * HG)
                        if c == TT - 1 and g + 1 < NG:
                            for j in range(HG):
                                spread(g + 1, j)
                        if c == 0 and g > 0:
                            pe.wait_ge(num_drained, START + b * (NG + 1) + g)
                        for j in range(HG):
                            f = (g * HG + j) * DH1
                            nc.tensor.matmul(acc[0][j * DH1:(j + 1) * DH1], h_tok[:, c, f:f + DH1],
                                             edge[:, (n * HG + j) % 8], start=(c == 0), stop=(c == TT - 1),
                                             skip_group_check=True)
                        for j in range(HG):
                            ins = nc.tensor.matmul(acc[1][j * DH1:(j + 1) * DH1], onehot_f[:, g],
                                                   edge[:, (n * HG + j) % 8], start=(n == 0),
                                                   stop=(n == NG * TT - 1), skip_group_check=True)
                        ins.then_inc(agg_done, 1)
                pe.wait_ge(num_drained, START + (b + 1) * (NG + 1))
                for t in range(TT):
                    u = W_FIN + t
                    work_free(pe, b, u)
                    for g in range(NG):
                        nc.tensor.transpose(work[u % 2][:, g * P:(g + 1) * P], numT[:, g, t * P:(t + 1) * P],
                                            ident_f[:])
                    nc.tensor.transpose(work[u % 2][:, D:N], denT[:, t * P:(t + 1) * P],
                                        ident_f[:]).then_inc(work_full, 1)


def host_layout(a):
    def rep(v):
        return np.ascontiguousarray(np.broadcast_to(v, (P, D)))

    wsd = np.zeros((D, ROWS), np.float32)
    for h in range(NH1):
        wsd[h * DH1:(h + 1) * DH1, h] = a["L1_gnn_w_src"][h, :, 0]
        wsd[h * DH1:(h + 1) * DH1, DROW + h] = a["L1_gnn_w_dst"][h, :, 0]
    sel = np.zeros((P, NH1, P), np.float32)
    onehot = np.zeros((P, NG, DH1), np.float32)
    for h in range(NH1):
        sel[h, h, :] = 1.0
        sel[DROW + h, h, :] = 1.0
    for g in range(NG):
        onehot[:, g, g] = 1.0
    return {
        "x": a["x"], "adj": a["adj"],
        "wq": a["L0_gnn_Wq"], "wk": a["L0_gnn_Wk"], "wv": a["L0_gnn_Wv"], "wf": a["L0_gnn_Wf"],
        "w1": a["L1_gnn_W"].transpose(1, 0, 2).reshape(D, D), "hw": a["L1_gnn_H_w"].T,
        "bqk": np.concatenate([a["L0_gnn_bq"].reshape(FC, P).T, a["L0_gnn_bk"].reshape(FC, P).T], axis=1),
        "bv": rep(a["L0_gnn_bv"]), "bf": rep(a["L0_gnn_bf"]),
        "b1": rep(np.tile(a["L1_gnn_b"], NH1)), "hb": rep(a["L1_gnn_H_b"]),
        "wsd": wsd, "ident": np.eye(P, dtype=np.float32),
        "sel": sel.reshape(P, NH1 * P), "onehot": onehot.reshape(P, NG * DH1),
    }


def kernel(**inputs):
    import concourse.bacc as bacc
    from concourse.bass_utils import run_bass_kernel_spmd

    arrays = host_layout({k: np.asarray(v) for k, v in inputs.items()})
    nc = bacc.Bacc("TRN2", target_bir_lowering=False, num_devices=1)
    feed, aps = {}, {}
    for name, v in arrays.items():
        v = np.ascontiguousarray(v)
        feed["in_" + name] = v
        aps[name] = nc.dram_tensor("in_" + name, v.shape, mybir.dt.from_np(v.dtype), kind="ExternalInput").ap()
    out = nc.dram_tensor("out_x", (B, N, D), F32, kind="ExternalOutput").ap()
    build(nc, **aps, out=out)
    r = run_bass_kernel_spmd(nc, [feed], core_ids=[0])
    return r.results[0]["out_x"]
```

```python
from contextlib import ExitStack

import numpy as np
import concourse.bass as bass
from concourse import mybir

F32 = mybir.dt.float32
F32R = mybir.dt.float32r
BF16 = mybir.dt.bfloat16
U8 = mybir.dt.uint8
ALU = mybir.AluOpType
ACT = mybir.ActivationFunctionType
AX_X = mybir.AxisListType.X

START = 1
B, N, D = 16, 512, 384
P = 128
TT = N // P
FC = D // P
NH0, DH0 = 6, 64
NPAIR = NH0 // 2
NH1, DH1 = 12, 32
HG = P // DH1
NG = NH1 // HG
EPS = 1e-5
NEG = 9000000000000000.0
SCALE = 1.0 / DH0 ** 0.5
LEAKY = 0.2
DROW = 32
ROWS = DROW + NH1

def named(name, n):
    return [(name, i) for i in range(n)]


OPEN = named("norm1", TT) + [("q", 0), ("k", 0), ("q", 1), ("k", 1)] + named("v", TT)
OWN = ([("q", 2), ("k", 2)] + named("adj", TT) + named("out", TT) + named("norm2", TT) + named("feat", FC)
       + [("tok", 0), ("tok", 1), ("rows", 0), ("tok", 2), ("tok", 3)] + named("gate", TT))
FIRST = OPEN
TURN = OWN + OPEN + named("fin", TT)
LAST = OWN + named("fin", TT)
assert len(FIRST) % 2 == 0 and len(TURN) % 2 == 0


def place(g, *name):
    last = isinstance(g, int) and g == B - 1
    if name not in FIRST:
        at, turns = (LAST if last else TURN).index(name), g
    elif isinstance(g, int) and g == 0:
        at, turns = FIRST.index(name) - len(FIRST), 0
    else:
        at, turns = TURN.index(name), g - 1
    at += len(FIRST)
    return at % 2, turns * (len(TURN) // 2) + at // 2, turns * len(TURN) + at


def build(nc, x, adj, wq, wk, wv, wf, w1, hw, bqk, bv, bf, b1, hb, wsd, ident, pick_in, onehot, out):
    with ExitStack() as ctx:
        def sb(name, shape, dt=F32):
            return ctx.enter_context(nc.sbuf_tensor(name, shape, dt))

        def sem(name):
            return ctx.enter_context(nc.semaphore(name))

        names = ["wq", "wk", "wv", "wf", "w1", "hw"]
        w_dram = dict(zip(names, [wq, wk, wv, wf, w1, hw]))
        w_hi = {n: sb(n + "_hi", [P, FC, D], F32R) for n in names}
        w_lo = {n: sb(n + "_lo", [P, FC, D], F32R) for n in names}
        ident_f = sb("ident_f", [P, P])
        ident_b = sb("ident_b", [P, P], BF16)
        pick = sb("pick", [P, NH1], F32R)
        onehot_f = sb("onehot_f", [P, NG, DH1])
        bias_qk = sb("bias_qk", [P, 2 * NPAIR])
        bias_v, bias_f, bias_h = (sb(n, [P, D]) for n in ("bias_v", "bias_f", "bias_h"))
        bias_1 = sb("bias_1", [P, DH1])
        wsd_f = sb("wsd_f", [P, FC, ROWS])

        x_in = sb("x_in", [P, TT, D])
        adj_u8 = sb("adj_u8", [P, TT, N], U8)
        xres = sb("xres", [P, TT, D])
        hn = sb("hn", [P, TT, D])
        mask = sb("mask", [P, TT, N], BF16)
        adjT = sb("adjT", [P, TT, N], BF16)
        hT_hi = sb("hT_hi", [P, FC, N], F32R)
        hT_lo = sb("hT_lo", [P, FC, N], F32R)
        stats = sb("stats", [P, TT, 6])
        mv = sb("mv", [P, TT, 2])
        var = sb("var", [P, TT])
        rstd = sb("rstd", [P, TT])
        shift = sb("shift", [P, TT])
        mhalf = sb("mhalf", [P, TT])
        qs = sb("qs", [P, 2, 2, N], F32R)
        kh = sb("kh", [P, 2, 2, N], F32R)
        kl = sb("kl", [P, 2, 2, N], F32R)
        qk_f = sb("qk_f", [P, 2, N])
        v_tok = sb("v_tok", [P, TT, D])
        ctx_hi = sb("ctx_hi", [P, NPAIR, N], F32R)
        ctx_lo = sb("ctx_lo", [P, NPAIR, N], F32R)
        nmax = sb("nmax", [P, NH0, TT])
        rsum = sb("rsum", [P, NH0, TT])
        rinv = sb("rinv", [P, NH0, TT])
        r_rows = sb("r_rows", [P, N], F32R)
        uv_rows = sb("uv_rows", [ROWS, N])
        dstat = sb("dstat", [ROWS, 4])
        uvT = sb("uvT", [P, TT, ROWS])
        nvT = sb("nvT", [P, TT, ROWS])
        rden = sb("rden", [P, 2, NG, HG])

        KB = 256
        arena = sb("arena", [P, 50 * KB])

        def view(start_kb, *shape):
            n = int(np.prod(shape))
            v = arena[:, int(start_kb * KB):int(start_kb * KB) + n]
            if len(shape) == 1:
                return v
            names_ = "abc"[:len(shape)]
            return v.rearrange("p (%s) -> p %s" % (" ".join(names_), " ".join(names_)),
                               **{c: s for c, s in zip(names_, shape)})

        pT = [view(0, TT, N), view(18, TT, N)]
        sm = view(14, 2, N)
        probs = view(26, 2 * TT, N)
        feat = view(0, FC, N)
        gate = view(0, TT, D)
        th = view(6, FC, N)
        numT = view(6, NG, N)
        h_tok = view(12, TT, D)
        t_ring = view(18, 4, N)
        edge = view(26, 8, N)
        denT = view(42, N)
        fin_f = view(44, 2, D)
        fin_q = view(47, 2, D)
        dd_rows = view(42, N)[0:ROWS]
        x_rows = view(44, N)[0:NH1]
        r_full = view(46, N)[0:NH1]
        stage = [view(4.5 * i, FC, D) for i in range(6)]
        pick_stage = view(30, NH1)

        def bank(name):
            return ctx.enter_context(nc.psum_tensor(name, [P, N], F32))

        work = [bank("work0"), bank("work1")]
        score = [bank("score0"), bank("score1")]
        turn = [bank("turn0"), bank("turn1")]
        acc = [bank("acc0"), bank("acc1")]
        rbank = score + turn

        consts_in = sem("consts_in")
        split_hi = sem("split_hi")
        setup_done = sem("setup_done")
        pool_setup = sem("pool_setup")
        x_loaded = sem("x_loaded")
        adj_loaded = sem("adj_loaded")
        res_loaded = sem("res_loaded")
        out_stored = sem("out_stored")
        stat_ready = sem("stat_ready")
        var_ready = sem("var_ready")
        rstd_ready = sem("rstd_ready")
        shift_ready = sem("shift_ready")
        hn_ready = sem("hn_ready")
        xb_ready = sem("xb_ready")
        mask_ready = sem("mask_ready")
        work_full = sem("work_full")
        work_drained = [sem("work_drained0"), sem("work_drained1")]
        hi_ready = sem("hi_ready")
        qk_ready = sem("qk_ready")
        score_full = sem("score_full")
        smax_ready = sem("smax_ready")
        exp_ready = sem("exp_ready")
        rinv_ready = sem("rinv_ready")
        probs_ready = sem("probs_ready")
        turn_full = sem("turn_full")
        pT_ready = [sem("pT_ready0"), sem("pT_ready1")]
        ctx_full = sem("ctx_full")
        ctx_ready = sem("ctx_ready")
        h2_used = sem("h2_used")
        h2p_ready = sem("h2p_ready")
        tanh_ready = sem("tanh_ready")
        gate_ready = sem("gate_ready")
        dstat_step = sem("dstat_step")
        rows_ready = sem("rows_ready")
        rlo_ready = sem("rlo_ready")
        uv_full = sem("uv_full")
        uv_ready = sem("uv_ready")
        r_spread = sem("r_spread")
        t_ready = sem("t_ready")
        edge_ready = sem("edge_ready")
        agg_done = sem("agg_done")
        num_drained = sem("num_drained")
        rden_ready = sem("rden_ready")
        pos_ready = sem("pos_ready")
        elu_exp = sem("elu_exp")
        diff_ready = sem("diff_ready")
        gated = sem("gated")
        out_ready = sem("out_ready")

        waits_passed = {e.engine: sem(f"waits_passed{i}")
                        for i, e in enumerate((nc.sync, nc.gpsimd, nc.vector, nc.tensor))}

        NCONST = 6 + 9

        def bank_of(g, *name):
            return work[place(g, *name)[0]]

        def mark_drained(ins, g, *name):
            ins.then_inc(work_drained[place(g, *name)[0]], 1)

        def drained(eng, g, *name):
            bank, before, _ = place(g, *name)
            eng.wait_ge(work_drained[bank], START + before + 1)

        def work_free(eng, g, *name):
            bank, before, _ = place(g, *name)
            eng.wait_ge(work_drained[bank], START + before)

        def prime(eng, *sems):
            for s in sems:
                eng.sem_inc(s, START)

        def settle(eng):
            eng.sem_inc(waits_passed[eng.engine], 1)

        def filled(eng, g, *name):
            eng.wait_ge(work_full, place(g, *name)[2] + 1)

        HI = 2 * TT + NPAIR
        STEPS = NG * TT

        block = ctx.enter_context(nc.Block())

        @block.sync
        def _(sp):
            for n, s in zip(names, stage):
                sp.dma_start(s, w_dram[n].rearrange("(c p) n -> p c n", p=P)).then_inc(consts_in, 16)
            for dst, src in ((ident_f[:], ident), (pick_stage, pick_in),
                             (onehot_f[:], onehot.rearrange("p (g m) -> p g m", g=NG)), (bias_qk[:], bqk),
                             (bias_v[:], bv), (bias_f[:], bf), (bias_1[:], b1), (bias_h[:], hb),
                             (wsd_f[:], wsd.rearrange("(c p) n -> p c n", p=P))):
                sp.dma_start(dst, src).then_inc(consts_in, 16)

            def load_x(b):
                sp.dma_start(x_in[:], x[b].rearrange("(t p) d -> p t d", p=P)).then_inc(x_loaded, 16)

            def load_adj(b):
                sp.dma_start(adj_u8[:], adj[b].rearrange("(t p) n -> p t n", p=P)).then_inc(adj_loaded, 16)

            def load_res(b):
                sp.dma_start(xres[:], x[b].rearrange("(t p) d -> p t d", p=P)).then_inc(res_loaded, 16)

            def store(b):
                for t in range(TT):
                    sp.wait_ge(out_ready, START + b * TT + t + 1)
                    settle(sp)
                    sp.dma_start(out[b, t * P:(t + 1) * P, :], xres[:, t]).then_inc(out_stored, 16)

            load_x(0)
            load_adj(0)
            load_res(0)
            with sp.Fori(0, B - 1) as b:
                sp.wait_ge(hi_ready, b * HI + TT)
                settle(sp)
                load_x(b + 1)
                sp.wait_ge(mask_ready, b + 1)
                settle(sp)
                load_adj(b + 1)
                store(b)
                sp.wait_ge(out_stored, START + (b + 1) * 16 * TT)
                settle(sp)
                load_res(b + 1)
            store(B - 1)
            sp.wait_ge(out_stored, START + B * 16 * TT)

        @block.gpsimd
        def _(pool):
            prime(pool, out_stored, out_ready)
            nc.gpsimd.memset(mhalf[:], -0.5).then_inc(pool_setup, 1)
            nc.gpsimd.memset(uv_rows[:], 0.0).then_inc(pool_setup, 1)
            pool.wait_ge(pool_setup, 2)

            def make_mask(g):
                pool.wait_ge(adj_loaded, 16 * g + 16)
                settle(pool)
                for t in range(TT):
                    ins = nc.gpsimd.tensor_scalar(mask[:, t], adj_u8[:, t], -NEG, NEG, ALU.mult, ALU.add)
                ins.then_inc(mask_ready, 1)

            def normalise(g, h):
                pool.wait_ge(rinv_ready, START + g * NH0 + h + 1)
                settle(pool)
                for t in range(TT):
                    pr = probs[:, (h % 2) * TT + t]
                    nc.gpsimd.tensor_scalar(pr, pr, rinv[:, h, t:t + 1], 1.0,
                                            ALU.mult, ALU.mult).then_inc(probs_ready, 1)

            def root(g, k):
                for half in range(2):
                    pool.wait_ge(var_ready, (2 * g + k) * 2 + half + 1)
                    s = slice(2 * half, 2 * half + 2)
                    nc.gpsimd.tensor_tensor(rstd[:, s], var[:, s], mhalf[:, s], ALU.pow).then_inc(rstd_ready, 1)

            def add_out(g, t):
                pool.wait_ge(gated, START + g * TT + t + 1)
                nc.gpsimd.tensor_tensor(xres[:, t], fin_q[:, t % 2], xres[:, t], ALU.add).then_inc(out_ready, 1)

            def graph(b, more):
                normalise(b, 2)
                normalise(b, 3)
                pool.wait_ge(res_loaded, 16 * b + 16)
                for t in range(TT):
                    ins = nc.gpsimd.tensor_tensor(xres[:, t], xres[:, t], bias_f[:], ALU.add)
                ins.then_inc(xb_ready, 1)
                normalise(b, 4)
                normalise(b, 5)
                root(b, 1)
                for t in range(TT):
                    pool.wait_ge(hn_ready, (2 * b + 1) * TT + t + 1)
                    nc.gpsimd.tensor_tensor(xres[:, t], xres[:, t], hn[:, t], ALU.add).then_inc(h2_used, 1)
                filled(pool, b, "norm2", TT - 1)
                pool.wait_ge(h2_used, (b + 1) * TT)
                settle(pool)
                for t in range(TT):
                    nc.gpsimd.tensor_scalar(hn[:, t], hn[:, t], 1.0, 1.0, ALU.add, ALU.mult).then_inc(h2p_ready, 1)
                if more:
                    root(b + 1, 0)
                    filled(pool, b, "adj", TT - 1)
                    make_mask(b + 1)
                for t in range(TT):
                    pool.wait_ge(tanh_ready, b * TT + t + 1)
                    settle(pool)
                    nc.gpsimd.tensor_scalar(gate[:, t], gate[:, t], 1.0, 1.0, ALU.add, ALU.mult).then_inc(gate_ready, 1)
                add_out(b, 0)
                add_out(b, 1)
                if more:
                    normalise(b + 1, 0)
                add_out(b, 2)
                add_out(b, 3)
                if more:
                    normalise(b + 1, 1)

            make_mask(0)
            root(0, 0)
            normalise(0, 0)
            normalise(0, 1)
            with pool.Fori(0, B - 1) as b:
                graph(b, True)
            graph(B - 1, False)

        @block.scalar
        def _(act):
            prime(act, t_ready, num_drained, pT_ready[1])
            act.wait_ge(consts_in, 16 * NCONST)
            for n, s in zip(names, stage):
                nc.scalar.activation(w_hi[n][:], s, ACT.Copy).then_inc(split_hi, 1)
            act.wait_ge(setup_done, 1)

            def norm(g, k, half):
                act.wait_ge(shift_ready, (2 * g + k) * 2 + half + 1)
                for t in (2 * half, 2 * half + 1):
                    nc.scalar.activation((hn if k else x_in)[:, t], x_res_or_in(k)[:, t], ACT.Relu,
                                         bias=shift[:, t:t + 1], scale=rstd[:, t:t + 1]).then_inc(hn_ready, 1)

            def x_res_or_in(k):
                return xres if k else x_in

            def turned_high(g, name, t):
                filled(act, g, name, t)
                nc.scalar.activation(hT_hi[:, :, t * P:(t + 1) * P],
                                     bank_of(g, name, t)[:, 0:D].rearrange("p (c n) -> p c n", c=FC),
                                     ACT.Copy).then_inc(hi_ready, 1)

            def qk_copy(g, p, name):
                s, w = p % 2, "qk".index(name)
                filled(act, g, name, p)
                ps = bank_of(g, name, p)
                act.wait_ge(qk_ready, START + g * NPAIR + p)

                def put(dst, lo, hi):
                    col = w * NPAIR + p
                    return nc.scalar.activation(dst, ps[lo:hi], ACT.Identity, scale=(-SCALE, 1.0)[w],
                                                bias=bias_qk[lo:hi, col:col + 1])
                put(qk_f[:, w], 0, P)
                for i in range(2):
                    lo, hi = i * DH0, (i + 1) * DH0
                    if w == 0:
                        last = put(qs[lo:hi, s, i], lo, hi)
                    else:
                        put(kh[0:DH0, s, i], lo, hi)
                        last = put(kh[DH0:P, s, i], lo, hi)
                mark_drained(last, g, name, p)

            def exps(g, h, tiles=range(TT)):
                for t in tiles:
                    i = h * TT + t
                    act.wait_ge(smax_ready, START + g * NH0 * TT + i + 1)
                    if t == 0 and h >= 2:
                        act.wait_ge(turn_full, (g * NH0 + h - 1) * TT)
                    if t == 0:
                        act.wait_ge(rinv_ready, START + g * NH0)
                    nc.scalar.activation(probs[:, (h % 2) * TT + t], sm[:, i % 2], ACT.Exp, scale=-1.0,
                                         bias=nmax[:, h, t:t + 1],
                                         accum_out=rsum[:, h, t:t + 1]).then_inc(exp_ready, 1)

            def pT_copy(b, h):
                if h == 0:
                    act.wait_ge(gated, START + b * TT)
                if h >= 2:
                    act.wait_ge(ctx_full, b * NPAIR + h // 2)
                for c in (1, 3):
                    act.wait_ge(turn_full, (b * NH0 + h) * TT + c + 1)
                    nc.scalar.activation(pT[h % 2][:, c], turn[1][:], ACT.Copy).then_inc(pT_ready[1], 1)

            def ctx_high(b, p):
                act.wait_ge(ctx_full, b * NPAIR + p + 1)
                nc.scalar.activation(ctx_hi[:, p], acc[p % 2][:], ACT.Copy).then_inc(hi_ready, 1)

            def adj_copy(b, c):
                filled(act, b, "adj", c)
                act.wait_ge(edge_ready, START + b * NH1 * TT)
                mark_drained(nc.scalar.activation(adjT[:, c], bank_of(b, "adj", c)[:, 0:N // 2].bitcast(BF16),
                                                  ACT.Relu, scale=-1.0, bias=1.0), b, "adj", c)

            def elu(b, t):
                act.wait_ge(pos_ready, b * TT + t + 1)
                nc.scalar.activation(fin_f[:, t % 2], fin_f[:, t % 2], ACT.Exp).then_inc(elu_exp, 1)

            def relus(b, n):
                g, c = n // TT, n % TT
                for j in range(HG):
                    k = n * HG + j
                    if c == 0:
                        act.wait_ge(r_spread, b * NH1 + g * HG + j + 1)
                    if k >= 4:
                        act.wait_ge(edge_ready, START + b * NH1 * TT + k - 3)
                    a = g * HG + j
                    nc.scalar.activation(t_ring[:, k % 4], rbank[j][:], ACT.Relu, scale=uvT[:, c, a:a + 1],
                                         bias=nvT[:, c, DROW + a:DROW + a + 1]).then_inc(t_ready, 1)

            def sums_copy(b, g):
                act.wait_ge(agg_done, b * STEPS + (g + 1) * TT)
                nc.scalar.activation(numT[:, g], acc[0][:], ACT.Copy).then_inc(num_drained, 1)

            def graph(b, more):
                pT_copy(b, 0)
                exps(b, 2)
                qk_copy(b, 2, "q")
                qk_copy(b, 2, "k")
                pT_copy(b, 1)
                exps(b, 3)
                adj_copy(b, 0)
                adj_copy(b, 1)
                ctx_high(b, 0)
                adj_copy(b, 2)
                adj_copy(b, 3)
                pT_copy(b, 2)
                exps(b, 4)
                pT_copy(b, 3)
                exps(b, 5)
                ctx_high(b, 1)
                pT_copy(b, 4)
                pT_copy(b, 5)
                ctx_high(b, 2)
                for half in range(2):
                    norm(b, 1, half)
                    for t in (2 * half, 2 * half + 1):
                        turned_high(b, "norm2", t)
                for c in range(FC):
                    filled(act, b, "feat", c)
                    ps = bank_of(b, "feat", c)
                    nc.scalar.activation(feat[:, c], ps[:], ACT.Copy)
                    mark_drained(nc.scalar.activation(th[:, c], ps[:], ACT.Tanh), b, "feat", c)
                drained(act, b, "rows", 0)
                nc.scalar.activation(uv_rows[0:NH1], dd_rows[DROW:ROWS], ACT.Exp)
                nc.scalar.activation(uv_rows[DROW:ROWS], dd_rows[DROW:ROWS], ACT.Exp,
                                     scale=LEAKY).then_inc(rows_ready, 1)
                nc.scalar.activation(r_full, x_rows, ACT.Exp, scale=1.0 - LEAKY)
                nc.scalar.activation(r_rows[0:NH1], x_rows, ACT.Exp, scale=1.0 - LEAKY).then_inc(rows_ready, 1)
                for t in range(TT):
                    drained(act, b, "gate", t)
                    nc.scalar.activation(gate[:, t], gate[:, t], ACT.Tanh, scale=0.5).then_inc(tanh_ready, 1)
                act.wait_ge(uv_ready, 2 * b + 2)
                for n in range(STEPS):
                    relus(b, n)
                    if n % TT == 0 and n > 0:
                        sums_copy(b, n // TT - 1)
                    if not more:
                        continue
                    if n in (1, 2):
                        norm(b + 1, 0, n - 1)
                    if n in (3, 4):
                        for t in (2 * n - 6, 2 * n - 5):
                            turned_high(b + 1, "norm1", t)
                    if n in (6, 7, 8, 9):
                        qk_copy(b + 1, (n - 6) // 2, "qk"[n % 2])
                sums_copy(b, NG - 1)
                nc.scalar.activation(denT, acc[1][:], ACT.Copy).then_inc(num_drained, 1)
                if more:
                    exps(b + 1, 0, (0, 1))
                for t in range(TT):
                    elu(b, t)
                    if more:
                        i = t + 2
                        exps(b + 1, i // TT, (i % TT,))
                if more:
                    exps(b + 1, 1, (2, 3))

            for half in range(2):
                norm(0, 0, half)
                for t in (2 * half, 2 * half + 1):
                    turned_high(0, "norm1", t)
            for p in range(2):
                qk_copy(0, p, "q")
                qk_copy(0, p, "k")
            exps(0, 0)
            exps(0, 1)
            with act.Fori(0, B - 1) as b:
                graph(b, True)
            graph(B - 1, False)

        @block.vector
        def _(dve):
            prime(dve, smax_ready, edge_ready, qk_ready, rinv_ready, gated, pT_ready[0], *work_drained)
            nc.vector.memset(r_rows[:].bitcast(F32), 0.0)
            nc.vector.memset(kl[:].bitcast(F32), 0.0)
            dve.wait_ge(consts_in, 16 * NCONST)
            nc.vector.tensor_copy(ident_b[:], ident_f[:])
            nc.vector.tensor_copy(pick[:], pick_stage)
            nc.vector.tensor_scalar(bias_qk[:, 0:NPAIR], bias_qk[:, 0:NPAIR], -SCALE, None, ALU.mult)
            for i, (n, s) in enumerate(zip(names, stage)):
                dve.wait_ge(split_hi, i + 1)
                ins = nc.vector.tensor_tensor(w_lo[n][:], s, w_hi[n][:].bitcast(F32), ALU.subtract)
            ins.then_inc(setup_done, 1)
            dve.wait_ge(setup_done, 1)

            def tile_stats(g, k, t, src):
                n0 = (2 * g + k) * 2 * TT + 2 * t
                nc.vector.bn_stats(stats[:, t], src[:, t]).then_inc(stat_ready, 1)
                dve.wait_ge(stat_ready, n0 + 1)
                settle(dve)
                nc.vector.bn_aggr(mv[:, t], stats[:, t]).then_inc(stat_ready, 1)

            def variance(g, k, half):
                dve.wait_ge(stat_ready, (2 * g + k) * 2 * TT + TT * (half + 1))
                s = slice(2 * half, 2 * half + 2)
                nc.vector.tensor_scalar(var[:, s], mv[:, s, 1], EPS, None, ALU.add).then_inc(var_ready, 1)

            def shifts(g, k, half):
                dve.wait_ge(rstd_ready, (2 * g + k) * 2 + half + 1)
                s = slice(2 * half, 2 * half + 2)
                nc.vector.scalar_tensor_tensor(out=shift[:, s], in0=mv[:, s, 0], scalar=-1.0, in1=rstd[:, s],
                                               op0=ALU.mult, op1=ALU.mult).then_inc(shift_ready, 1)

            def turned_low(g, k, name, t):
                dve.wait_ge(hi_ready, g * HI + k * (TT + NPAIR) + t + 1)
                s = slice(t * P, (t + 1) * P)
                mark_drained(nc.vector.tensor_tensor(
                    hT_lo[:, :, s], bank_of(g, name, t)[:, 0:D].rearrange("p (c n) -> p c n", c=FC),
                    hT_hi[:, :, s].bitcast(F32), ALU.subtract), g, name, t)

            def qk_low(g, p, name):
                s, w = p % 2, "qk".index(name)
                drained(dve, g, name, p)
                for i in range(2):
                    lo, hi = i * DH0, (i + 1) * DH0
                    o = (1 - i) * DH0
                    if w == 0:
                        nc.vector.tensor_tensor(qs[o:o + DH0, s, i], qk_f[lo:hi, 0], qs[lo:hi, s, i].bitcast(F32),
                                                ALU.subtract)
                    else:
                        ins = nc.vector.tensor_tensor(kl[lo:hi, s, i], qk_f[lo:hi, 1], kh[lo:hi, s, i].bitcast(F32),
                                                      ALU.subtract)
                if w == 1:
                    ins.then_inc(qk_ready, 1)

            def value(g, t):
                filled(dve, g, "v", t)
                mark_drained(nc.vector.tensor_tensor(v_tok[:, t], bank_of(g, "v", t)[:, 0:D], bias_v[:], ALU.add),
                             g, "v", t)

            def maxima(g, h, tiles=range(TT)):
                for t in tiles:
                    i = h * TT + t
                    dve.wait_ge(score_full, g * NH0 * TT + i + 1)
                    if i >= 2:
                        dve.wait_ge(exp_ready, g * NH0 * TT + i - 1)
                    settle(dve)
                    nc.vector.tensor_tensor_reduce(sm[:, i % 2], score[i % 2][:], mask[:, t], 1.0, 3.0e38,
                                                   ALU.add, ALU.min, nmax[:, h, t:t + 1]).then_inc(smax_ready, 1)

            def inverse(g, h):
                dve.wait_ge(exp_ready, (g * NH0 + h + 1) * TT)
                nc.vector.reciprocal(rinv[:, h], rsum[:, h]).then_inc(rinv_ready, 1)

            def pT_copy(b, h):
                if h >= 2:
                    dve.wait_ge(ctx_full, b * NPAIR + h // 2)
                for c in (0, 2):
                    dve.wait_ge(turn_full, (b * NH0 + h) * TT + c + 1)
                    nc.vector.tensor_copy(pT[h % 2][:, c], turn[0][:]).then_inc(pT_ready[0], 1)

            def ctx_low(b, p):
                dve.wait_ge(hi_ready, b * HI + TT + p + 1)
                nc.vector.tensor_tensor(ctx_lo[:, p], acc[p % 2][:], ctx_hi[:, p].bitcast(F32),
                                        ALU.subtract).then_inc(ctx_ready, 1)

            def residual(b, t):
                filled(dve, b, "out", t)
                mark_drained(nc.vector.tensor_tensor(xres[:, t], bank_of(b, "out", t)[:, 0:D], xres[:, t], ALU.add),
                             b, "out", t)
                drained(dve, b, "out", t)
                tile_stats(b, 1, t, xres)

            def token(b, t):
                filled(dve, b, "tok", t)
                heads = "p (a e) -> p a e"
                mark_drained(nc.vector.tensor_tensor(
                    h_tok[:, t].rearrange(heads, a=NH1), bank_of(b, "tok", t)[:, 0:D].rearrange(heads, a=NH1),
                    bias_1[:].unsqueeze(1).to_broadcast([P, NH1, DH1]), ALU.add), b, "tok", t)

            def gate_sum(b, t):
                filled(dve, b, "gate", t)
                mark_drained(nc.vector.tensor_tensor(gate[:, t], bank_of(b, "gate", t)[:, 0:D], bias_h[:], ALU.add),
                             b, "gate", t)

            def edges(b, n):
                g, c = n // TT, n % TT
                for j in range(HG):
                    k = n * HG + j
                    dve.wait_ge(t_ready, START + b * NH1 * TT + k + 1)
                    if j == 0 and n >= 2:
                        dve.wait_ge(agg_done, b * STEPS + n - 1)
                    a = DROW + g * HG + j
                    nc.vector.scalar_tensor_tensor(out=edge[:, k % 8], in0=t_ring[:, k % 4],
                                                   scalar=uvT[:, c, a:a + 1], in1=adjT[:, c],
                                                   op0=ALU.add, op1=ALU.mult).then_inc(edge_ready, 1)

            def divide(b, t):
                n = b * TT + t
                filled(dve, b, "fin", t)
                ps = bank_of(b, "fin", t)
                nc.vector.reciprocal(rden[:, t % 2], ps[:, D:N].rearrange("p (j s) -> p s j", j=HG)[:, 0:NG]
                                     ).then_inc(rden_ready, 1)
                dve.wait_ge(rden_ready, n + 1)
                mark_drained(nc.vector.tensor_tensor(
                    fin_f[:, t % 2].rearrange("p (a e) -> p a e", a=NH1),
                    ps[:, 0:D].rearrange("p (a e) -> p a e", a=NH1),
                    rden[:, t % 2].rearrange("p g j -> p (g j)").unsqueeze(2).to_broadcast([P, NH1, DH1]),
                    ALU.mult), b, "fin", t)
                drained(dve, b, "fin", t)
                dve.wait_ge(out_ready, START + n - 1 if t >= 2 else START + b * TT)
                nc.vector.scalar_tensor_tensor(out=fin_q[:, t % 2], in0=fin_f[:, t % 2], scalar=0.0, in1=hn[:, t],
                                               op0=ALU.max, op1=ALU.subtract).then_inc(pos_ready, 1)

            def gating(b, t):
                n = b * TT + t
                dve.wait_ge(elu_exp, n + 1)
                nc.vector.scalar_tensor_tensor(out=fin_f[:, t % 2], in0=fin_f[:, t % 2], scalar=1.0,
                                               in1=fin_q[:, t % 2], op0=ALU.min, op1=ALU.add).then_inc(diff_ready, 1)
                dve.wait_ge(diff_ready, n + 1)
                nc.vector.scalar_tensor_tensor(out=fin_q[:, t % 2], in0=fin_f[:, t % 2], scalar=0.5,
                                               in1=gate[:, t], op0=ALU.mult, op1=ALU.mult).then_inc(gated, 1)

            def graph(b, more):
                pT_copy(b, 0)
                maxima(b, 2)
                pT_copy(b, 1)
                maxima(b, 3, [0])
                inverse(b, 2)
                maxima(b, 3, range(1, TT))
                qk_low(b, 2, "q")
                qk_low(b, 2, "k")
                ctx_low(b, 0)
                pT_copy(b, 2)
                maxima(b, 4, [0])
                inverse(b, 3)
                maxima(b, 4, range(1, TT))
                pT_copy(b, 3)
                maxima(b, 5, [0])
                inverse(b, 4)
                maxima(b, 5, range(1, TT))
                inverse(b, 5)
                ctx_low(b, 1)
                pT_copy(b, 4)
                pT_copy(b, 5)
                ctx_low(b, 2)
                dve.wait_ge(xb_ready, b + 1)
                residual(b, 0)
                residual(b, 1)
                variance(b, 1, 0)
                residual(b, 2)
                shifts(b, 1, 0)
                residual(b, 3)
                variance(b, 1, 1)
                shifts(b, 1, 1)
                for t in range(TT):
                    turned_low(b, 1, "norm2", t)
                token(b, 0)
                token(b, 1)
                s0 = b * 5
                filled(dve, b, "rows", 0)
                rows = bank_of(b, "rows", 0)
                nc.vector.tensor_reduce(dstat[DROW:ROWS, 0:1], rows[DROW:ROWS], AX_X, ALU.max).then_inc(dstat_step, 1)
                nc.vector.tensor_reduce(dstat[DROW:ROWS, 1:2], rows[DROW:ROWS], AX_X, ALU.min).then_inc(dstat_step, 1)
                dve.wait_ge(dstat_step, s0 + 2)
                nc.vector.tensor_tensor(dstat[DROW:ROWS, 1:2], dstat[DROW:ROWS, 0:1], dstat[DROW:ROWS, 1:2],
                                        ALU.subtract).then_inc(dstat_step, 1)
                dve.wait_ge(dstat_step, s0 + 3)
                nc.vector.tensor_copy(dstat[0:NH1, 0:2], dstat[DROW:ROWS, 0:2]).then_inc(dstat_step, 1)
                nc.vector.tensor_scalar(dd_rows[DROW:ROWS], rows[DROW:ROWS], dstat[DROW:ROWS, 0:1], None,
                                        ALU.subtract).then_inc(dstat_step, 1)
                dve.wait_ge(dstat_step, s0 + 5)
                mark_drained(nc.vector.tensor_scalar(x_rows, rows[0:NH1], dstat[0:NH1, 0:1], dstat[0:NH1, 1:2],
                                                     ALU.add, ALU.min), b, "rows", 0)
                token(b, 2)
                token(b, 3)
                gate_sum(b, 0)
                dve.wait_ge(rows_ready, 2 * b + 2)
                nc.vector.tensor_tensor(r_rows[DROW:ROWS], r_full, r_rows[0:NH1].bitcast(F32),
                                        ALU.subtract).then_inc(rlo_ready, 1)
                gate_sum(b, 1)
                dve.wait_ge(uv_full, b + 1)
                uv_ps = score[0][:, 0:TT * ROWS].rearrange("p (c r) -> p c r", c=TT)
                nc.vector.tensor_copy(uvT[:], uv_ps).then_inc(uv_ready, 1)
                nc.vector.tensor_scalar(nvT[:], uv_ps, -1.0, None, ALU.mult).then_inc(uv_ready, 1)
                gate_sum(b, 2)
                gate_sum(b, 3)
                dve.wait_ge(uv_ready, 2 * b + 2)
                if more:
                    dve.wait_ge(x_loaded, 16 * b + 32)
                    tile_stats(b + 1, 0, 0, x_in)
                    tile_stats(b + 1, 0, 1, x_in)
                    variance(b + 1, 0, 0)
                for n in range(STEPS):
                    edges(b, n)
                    if not more:
                        continue
                    if n == 0:
                        shifts(b + 1, 0, 0)
                        tile_stats(b + 1, 0, 2, x_in)
                        tile_stats(b + 1, 0, 3, x_in)
                        variance(b + 1, 0, 1)
                    if n == 1:
                        shifts(b + 1, 0, 1)
                    if n in (3, 4):
                        for t in (2 * n - 6, 2 * n - 5):
                            turned_low(b + 1, 0, "norm1", t)
                    if n in (6, 7, 8, 9):
                        qk_low(b + 1, (n - 6) // 2, "qk"[n % 2])
                    if n >= 9:
                        value(b + 1, n - 9)
                if more:
                    value(b + 1, TT - 1)
                    dve.wait_ge(agg_done, (b + 1) * STEPS)
                    dve.wait_ge(mask_ready, b + 2)
                    maxima(b + 1, 0, (0, 1))
                dve.wait_ge(gate_ready, (b + 1) * TT)
                dve.wait_ge(h2p_ready, (b + 1) * TT)
                divide(b, 0)
                for t in range(1, TT):
                    if more:
                        maxima(b + 1, (t + 1) // TT, ((t + 1) % TT,))
                        if t == 3:
                            inverse(b + 1, 0)
                    divide(b, t)
                    gating(b, t - 1)
                if more:
                    maxima(b + 1, 1, (1,))
                gating(b, TT - 1)
                if more:
                    maxima(b + 1, 1, (2, 3))
                    inverse(b + 1, 1)

            dve.wait_ge(x_loaded, 16)
            for half in range(2):
                for t in (2 * half, 2 * half + 1):
                    tile_stats(0, 0, t, x_in)
                variance(0, 0, half)
            for half in range(2):
                shifts(0, 0, half)
            for t in range(TT):
                turned_low(0, 0, "norm1", t)
            for p in range(2):
                qk_low(0, p, "q")
                qk_low(0, p, "k")
            for t in range(TT):
                value(0, t)
            dve.wait_ge(mask_ready, 1)
            maxima(0, 0)
            maxima(0, 1, [0])
            inverse(0, 0)
            maxima(0, 1, range(1, TT))
            inverse(0, 1)
            with dve.Fori(0, B - 1) as b:
                graph(b, True)
            graph(B - 1, False)

        @block.tensor
        def _(pe):
            pe.wait_ge(setup_done, 1)

            def three(ps, l_hi, l_lo, r_hi, r_lo):
                n = 0
                for c in range(FC):
                    for l, r in ((l_hi, r_hi), (l_hi, r_lo), (l_lo, r_hi)):
                        ins = nc.tensor.matmul(ps, l(c), r(c), start=(n == 0), stop=(n == 3 * FC - 1))
                        n += 1
                return ins

            def cols(t, lo, hi=None):
                return lambda c: t[:, c, lo:lo + P]

            def whole(t):
                return lambda c: t[:, c, :]

            def turn_norm(g, k, name, t):
                work_free(pe, g, name, t)
                pe.wait_ge(hn_ready, (2 * g + k) * TT + t + 1)
                for c in range(FC):
                    ins = nc.tensor.transpose(bank_of(g, name, t)[:, c * P:(c + 1) * P],
                                              (hn if k else x_in)[:, t, c * P:(c + 1) * P], ident_f[:])
                ins.then_inc(work_full, 1)

            def by_feature(g, name, w, c):
                work_free(pe, g, name, c)
                three(bank_of(g, name, c)[:], cols(w_hi[w], c * P), cols(w_lo[w], c * P), whole(hT_hi),
                      whole(hT_lo)).then_inc(work_full, 1)

            def by_node(g, name, l_hi, l_lo, w, t):
                work_free(pe, g, name, t)
                three(bank_of(g, name, t)[:, 0:D], cols(l_hi, t * P), cols(l_lo, t * P), whole(w_hi[w]),
                      whole(w_lo[w])).then_inc(work_full, 1)

            def hT_ready(g, name):
                drained(pe, g, name, TT - 2)
                drained(pe, g, name, TT - 1)

            def query_key(g, p, name):
                by_feature(g, name, "w" + name, p)

            def values(g, t):
                by_node(g, "v", hT_hi, hT_lo, "wv", t)

            def scores(g, h, tiles=range(TT)):
                s, i = (h // 2) % 2, h % 2
                for t in tiles:
                    n = h * TT + t
                    if i == 0 and t == 0:
                        pe.wait_ge(qk_ready, START + g * NPAIR + h // 2 + 1)
                    if n < 2:
                        pe.wait_ge(t_ready, START + g * NH1 * TT)
                    else:
                        pe.wait_ge(smax_ready, START + g * NH0 * TT + n - 1)
                    q = qs[:, s, i, t * P:(t + 1) * P]
                    nc.tensor.matmul(score[n % 2][:], q, kh[:, s, i], start=True, stop=False)
                    nc.tensor.matmul(score[n % 2][:], q, kl[:, s, i], start=False, stop=True).then_inc(score_full, 1)

            def turn_probs(b, h):
                for c in range(TT):
                    n = h * TT + c
                    for t in range(TT):
                        if c == 0:
                            pe.wait_ge(probs_ready, b * NH0 * TT + h * TT + t + 1)
                        if t == 0:
                            pe.wait_ge(pT_ready[c % 2], START + b * NH0 * 2 + n // 2)
                        ins = nc.tensor.transpose(turn[c % 2][:, t * P:(t + 1) * P],
                                                  probs[:, (h % 2) * TT + t, c * P:(c + 1) * P], ident_f[:])
                    ins.then_inc(turn_full, 1)

            def context(b, p):
                if p == 0:
                    pe.wait_ge(num_drained, START + b * (NG + 1))
                if p == 2:
                    pe.wait_ge(ctx_ready, b * NPAIR + 1)
                for c in range(TT):
                    pe.wait_ge(pT_ready[c % 2], START + b * NH0 * 2 + (2 * p + 1) * 2 + c // 2 + 1)
                    for i in range(2):
                        f = (2 * p + i) * DH0
                        ins = nc.tensor.matmul(acc[p % 2][i * DH0:(i + 1) * DH0], v_tok[:, c, f:f + DH0],
                                               pT[i][:, c], start=(c == 0), stop=(c == TT - 1))
                ins.then_inc(ctx_full, 1)

            def turn_adj(b, c):
                work_free(pe, b, "adj", c)
                for t in range(TT):
                    ins = nc.tensor.transpose(bank_of(b, "adj", c)[:, t * P // 2:(t + 1) * P // 2].bitcast(BF16),
                                              mask[:, t, c * P:(c + 1) * P], ident_b[:])
                ins.then_inc(work_full, 1)

            def turn_feat(b, t):
                work_free(pe, b, "tok", t)
                for c in range(FC):
                    ins = nc.tensor.transpose(bank_of(b, "tok", t)[:, c * P:(c + 1) * P],
                                              feat[:, c, t * P:(t + 1) * P], ident_f[:])
                ins.then_inc(work_full, 1)

            def spread(b, g, j):
                if g > 0:
                    pe.wait_ge(t_ready, START + b * NH1 * TT + (g * TT - 1) * HG + j + 1)
                h = g * HG + j
                nc.tensor.matmul(rbank[j][:], pick[:, h:h + 1].to_broadcast([P, P]), r_rows[:], start=True,
                                 stop=True).then_inc(r_spread, 1)

            def aggregate(b, n):
                g, c = n // TT, n % TT
                pe.wait_ge(edge_ready, START + b * NH1 * TT + (n + 1) * HG)
                if c == 0 and g > 0:
                    pe.wait_ge(num_drained, START + b * (NG + 1) + g)
                for j in range(HG):
                    f = (g * HG + j) * DH1
                    nc.tensor.matmul(acc[0][j * DH1:(j + 1) * DH1], h_tok[:, c, f:f + DH1],
                                     edge[:, (n * HG + j) % 8], start=(c == 0), stop=(c == TT - 1),
                                     skip_group_check=True)
                for j in range(HG):
                    ins = nc.tensor.matmul(acc[1][j * DH1:(j + 1) * DH1], onehot_f[:, g],
                                           edge[:, (n * HG + j) % 8], start=(n == 0),
                                           stop=(n == STEPS - 1), skip_group_check=True)
                ins.then_inc(agg_done, 1)

            def turn_sums(b, t):
                if t == 0:
                    pe.wait_ge(num_drained, START + (b + 1) * (NG + 1))
                work_free(pe, b, "fin", t)
                ps = bank_of(b, "fin", t)
                for g in range(NG):
                    nc.tensor.transpose(ps[:, g * P:(g + 1) * P], numT[:, g, t * P:(t + 1) * P], ident_f[:])
                nc.tensor.transpose(ps[:, D:N], denT[:, t * P:(t + 1) * P], ident_f[:]).then_inc(work_full, 1)

            def graph(b, more):
                turn_probs(b, 0)
                scores(b, 2)
                query_key(b, 2, "q")
                query_key(b, 2, "k")
                turn_probs(b, 1)
                scores(b, 3)
                turn_adj(b, 0)
                turn_adj(b, 1)
                context(b, 0)
                turn_adj(b, 2)
                turn_adj(b, 3)
                turn_probs(b, 2)
                scores(b, 4)
                turn_probs(b, 3)
                scores(b, 5)
                context(b, 1)
                turn_probs(b, 4)
                turn_probs(b, 5)
                context(b, 2)
                pe.wait_ge(ctx_ready, (b + 1) * NPAIR)
                for t in range(TT):
                    by_node(b, "out", ctx_hi, ctx_lo, "wf", t)
                for t in range(TT):
                    turn_norm(b, 1, "norm2", t)
                hT_ready(b, "norm2")
                for c in range(FC):
                    by_feature(b, "feat", "w1", c)
                drained(pe, b, "feat", 1)
                drained(pe, b, "feat", 2)
                turn_feat(b, 0)
                turn_feat(b, 1)
                work_free(pe, b, "rows", 0)
                for c in range(FC):
                    ins = nc.tensor.matmul(bank_of(b, "rows", 0)[0:ROWS], wsd_f[:, c], th[:, c], start=(c == 0),
                                           stop=(c == FC - 1))
                ins.then_inc(work_full, 1)
                turn_feat(b, 2)
                turn_feat(b, 3)
                by_node(b, "gate", hT_hi, hT_lo, "hw", 0)
                by_node(b, "gate", hT_hi, hT_lo, "hw", 1)
                pe.wait_ge(rows_ready, 2 * b + 1)
                settle(pe)
                for c in range(TT):
                    ins = nc.tensor.transpose(score[0][:, c * ROWS:(c + 1) * ROWS], uv_rows[:, c * P:(c + 1) * P],
                                              ident_f[0:ROWS, 0:ROWS])
                ins.then_inc(uv_full, 1)
                by_node(b, "gate", hT_hi, hT_lo, "hw", 2)
                pe.wait_ge(rlo_ready, b + 1)
                pe.wait_ge(uv_ready, 2 * b + 2)
                for j in range(HG):
                    spread(b, 0, j)
                by_node(b, "gate", hT_hi, hT_lo, "hw", 3)
                for n in range(STEPS):
                    if n % TT == TT - 1 and n < STEPS - 1:
                        for j in range(HG):
                            spread(b, n // TT + 1, j)
                    aggregate(b, n)
                    if not more:
                        continue
                    if n in (1, 2):
                        for t in (2 * n - 2, 2 * n - 1):
                            turn_norm(b + 1, 0, "norm1", t)
                    if n == 4:
                        hT_ready(b + 1, "norm1")
                    if n in (4, 5, 6, 7):
                        query_key(b + 1, (n - 4) // 2, "qk"[n % 2])
                    if n >= 8:
                        values(b + 1, n - 8)
                if more:
                    scores(b + 1, 0, (0, 1))
                for t in range(TT):
                    turn_sums(b, t)
                    if more:
                        scores(b + 1, (t + 2) // TT, ((t + 2) % TT,))
                if more:
                    scores(b + 1, 1, (2, 3))
                    drained(pe, b + 1, "v", TT - 1)

            for t in range(TT):
                turn_norm(0, 0, "norm1", t)
            hT_ready(0, "norm1")
            for p in range(2):
                query_key(0, p, "q")
                query_key(0, p, "k")
            for t in range(TT):
                values(0, t)
            scores(0, 0)
            scores(0, 1)
            drained(pe, 0, "v", TT - 2)
            drained(pe, 0, "v", TT - 1)
            with pe.Fori(0, B - 1) as b:
                graph(b, True)
            graph(B - 1, False)


def host_layout(a):
    def rep(v):
        return np.ascontiguousarray(np.broadcast_to(v, (P, D)))

    wsd = np.zeros((D, ROWS), np.float32)
    for h in range(NH1):
        wsd[h * DH1:(h + 1) * DH1, h] = a["L1_gnn_w_src"][h, :, 0]
        wsd[h * DH1:(h + 1) * DH1, DROW + h] = a["L1_gnn_w_dst"][h, :, 0]
    pick = np.zeros((P, NH1), np.float32)
    onehot = np.zeros((P, NG, DH1), np.float32)
    for h in range(NH1):
        pick[h, h] = 1.0
        pick[DROW + h, h] = 1.0
    for g in range(NG):
        onehot[:, g, g] = 1.0
    return {
        "x": a["x"], "adj": a["adj"],
        "wq": a["L0_gnn_Wq"], "wk": a["L0_gnn_Wk"], "wv": a["L0_gnn_Wv"], "wf": a["L0_gnn_Wf"],
        "w1": a["L1_gnn_W"].transpose(1, 0, 2).reshape(D, D), "hw": a["L1_gnn_H_w"].T,
        "bqk": np.concatenate([a["L0_gnn_bq"].reshape(FC, P).T, a["L0_gnn_bk"].reshape(FC, P).T], axis=1),
        "bv": rep(a["L0_gnn_bv"]), "bf": rep(a["L0_gnn_bf"]),
        "b1": np.broadcast_to(a["L1_gnn_b"], (P, DH1)), "hb": rep(a["L1_gnn_H_b"]),
        "wsd": wsd, "ident": np.eye(P, dtype=np.float32),
        "pick_in": pick, "onehot": onehot.reshape(P, NG * DH1),
    }


def kernel(**inputs):
    import concourse.bacc as bacc
    from concourse.bass_utils import run_bass_kernel_spmd

    arrays = host_layout({k: np.asarray(v) for k, v in inputs.items()})
    nc = bacc.Bacc("TRN2", target_bir_lowering=False, num_devices=1)
    feed, aps = {}, {}
    for name, v in arrays.items():
        v = np.ascontiguousarray(v)
        feed["in_" + name] = v
        aps[name] = nc.dram_tensor("in_" + name, v.shape, mybir.dt.from_np(v.dtype), kind="ExternalInput").ap()
    out = nc.dram_tensor("out_x", (B, N, D), F32, kind="ExternalOutput").ap()
    build(nc, **aps, out=out)
    r = run_bass_kernel_spmd(nc, [feed], core_ids=[0])
    return r.results[0]["out_x"]
```

```python
from contextlib import ExitStack

import numpy as np
import concourse.bass as bass
from concourse import mybir

F32 = mybir.dt.float32
F32R = mybir.dt.float32r
BF16 = mybir.dt.bfloat16
U8 = mybir.dt.uint8
ALU = mybir.AluOpType
ACT = mybir.ActivationFunctionType
AX_X = mybir.AxisListType.X

START = 1
B, N, D = 16, 512, 384
P = 128
TT = N // P
FC = D // P
NH0, DH0 = 6, 64
NPAIR = NH0 // 2
NH1, DH1 = 12, 32
HG = P // DH1
NG = NH1 // HG
EPS = 1e-5
NEG = 9000000000000000.0
SCALE = 1.0 / DH0 ** 0.5
LEAKY = 0.2
DROW = 32
ROWS = DROW + NH1

def named(name, n):
    return [(name, i) for i in range(n)]


OPEN = named("norm1", TT) + [("q", 0), ("k", 0), ("q", 1), ("k", 1), ("v", 0)]
OWN = ([("q", 2), ("k", 2), ("adj", 0), ("adj", 1)] + named("out", TT)
       + [("norm2", 0), ("norm2", 1), ("gate", 0), ("norm2", 2), ("norm2", 3), ("adj", 2), ("adj", 3)]
       + named("feat", FC) + named("tok", TT) + [("gate", 1), ("uq", 0), ("gate", 2), ("gate", 3)])
FIRST = OPEN + [("v", 1), ("v", 2), ("v", 3)]
TURN = OWN + OPEN + named("fin", TT) + [("v", 1), ("v", 2), ("v", 3)]
LAST = OWN + named("fin", TT)
assert FIRST[-2:] == TURN[-2:]
assert len(FIRST) % 2 == 0 and len(TURN) % 2 == 0


def place(g, *name):
    last = isinstance(g, int) and g == B - 1
    if name not in FIRST:
        at, turns = (LAST if last else TURN).index(name), g
    elif isinstance(g, int) and g == 0:
        at, turns = FIRST.index(name) - len(FIRST), 0
    else:
        at, turns = TURN.index(name), g - 1
    at += len(FIRST)
    return at % 2, turns * (len(TURN) // 2) + at // 2, turns * len(TURN) + at


def build(nc, x, adj, wq, wk, wv, wf, w1, hw, bc, bf, hb, wsd, ident, pick_in, out):
    with ExitStack() as ctx:
        def sb(name, shape, dt=F32):
            return ctx.enter_context(nc.sbuf_tensor(name, shape, dt))

        def sem(name):
            return ctx.enter_context(nc.semaphore(name))

        names = ["wq", "wk", "wv", "wf", "w1", "hw"]
        w_dram = dict(zip(names, [wq, wk, wv, wf, w1, hw]))
        w_hi = {n: sb(n + "_hi", [P, FC, D], F32R) for n in names}
        w_lo = {n: sb(n + "_lo", [P, FC, D], F32R) for n in names}
        ident_f = sb("ident_f", [P, P])
        ident_b = sb("ident_b", [P, P], BF16)
        pick = sb("pick", [P, NH1], F32R)
        bias_c = sb("bias_c", [P, 3 * NPAIR + 1])
        bias_f, bias_h = (sb(n, [P, D]) for n in ("bias_f", "bias_h"))
        wsd_f = sb("wsd_f", [P, FC, ROWS])

        x_in = sb("x_in", [P, TT, D])
        adj_u8 = sb("adj_u8", [P, TT, N], U8)
        xres = sb("xres", [P, TT, D])
        hn = sb("hn", [P, TT, D])
        mask = sb("mask", [P, TT, N], BF16)
        adjT = sb("adjT", [P, TT, N], BF16)
        hT_hi = sb("hT_hi", [P, FC, N], F32R)
        hT_lo = sb("hT_lo", [P, FC, N], F32R)
        stats = sb("stats", [P, TT, 6])
        mv = sb("mv", [P, TT, 2])
        var = sb("var", [P, TT])
        rstd = sb("rstd", [P, TT])
        shift = sb("shift", [P, TT])
        mhalf = sb("mhalf", [P, TT])
        qs = sb("qs", [P, 2, 2, N], F32R)
        kh = sb("kh", [P, 2, 2, N], F32R)
        kl = sb("kl", [P, 2, 2, N], F32R)
        sm = sb("sm", [P, 2, N])
        v_tok = sb("v_tok", [P, TT, D])
        fin_g = sb("fin_g", [P, D])
        ctx_hi = sb("ctx_hi", [P, NPAIR, N], F32R)
        ctx_lo = sb("ctx_lo", [P, NPAIR, N], F32R)
        nmax = sb("nmax", [P, NH0, TT])
        rsum = sb("rsum", [P, NH0, TT])
        rinv = sb("rinv", [P, NH0, TT])
        r_rows = sb("r_rows", [P, N], F32R)
        uq_rows = sb("uq_rows", [ROWS, N])
        dstat = sb("dstat", [ROWS, 4])
        uqT = sb("uqT", [P, TT, ROWS])
        nqT = sb("nqT", [P, TT, NH1])
        u_den = sb("u_den", [P, TT, NG, HG, DH1])
        rden = sb("rden", [P, 2, NG, HG])

        KB = 256
        arena = sb("arena", [P, 50 * KB])

        def view(start_kb, *shape):
            n = int(np.prod(shape))
            v = arena[:, int(start_kb * KB):int(start_kb * KB) + n]
            if len(shape) == 1:
                return v
            names_ = "abc"[:len(shape)]
            return v.rearrange("p (%s) -> p %s" % (" ".join(names_), " ".join(names_)),
                               **{c: s for c, s in zip(names_, shape)})

        pT_early = [view(18, TT, N), view(0, TT, N)]
        pT_late = [view(26, TT, N), view(34, TT, N)]
        probs = [view(26, TT, N), view(34, TT, N), view(42, TT, N)]
        feat = view(26, FC, N)
        gate = view(0, TT, D)
        th = view(6, FC, N)
        numT = view(6, NG, N)
        h_tok = view(12, TT, D)
        fin_q = view(12, TT, D)
        t_ring = view(18, 2, N)
        edge = view(26, 8, N)
        denT = view(42, N)
        fin_f = view(44, 2, D)
        dd_rows = view(42, N)[0:ROWS]
        x_rows = view(44, N)[0:NH1]
        r_full = view(46, N)[0:NH1]
        stage = {n: view(at, FC, D) for n, at in zip(names, (0, 4.5, 9, 13.5, 18, 42))}
        pick_stage = view(47, NH1)

        def bank(name):
            return ctx.enter_context(nc.psum_tensor(name, [P, N], F32))

        work = [bank("work0"), bank("work1")]
        score = [bank("score0"), bank("score1")]
        turn = [bank("turn0"), bank("turn1")]
        acc = [bank("acc0"), bank("acc1")]
        rbank = score + turn

        weight_in = {n: sem(n + "_in") for n in names}
        consts_in = sem("consts_in")
        consts_ready = sem("consts_ready")
        split_hi = sem("split_hi")
        split = sem("split")
        pool_setup = sem("pool_setup")
        x_loaded = sem("x_loaded")
        adj_loaded = sem("adj_loaded")
        res_loaded = sem("res_loaded")
        out_stored = sem("out_stored")
        stat_ready = sem("stat_ready")
        mean_ready = sem("mean_ready")
        var_ready = sem("var_ready")
        rstd_ready = sem("rstd_ready")
        shift_ready = sem("shift_ready")
        xn_ready = sem("xn_ready")
        hn_ready = sem("hn_ready")
        xb_ready = sem("xb_ready")
        mask_ready = sem("mask_ready")
        work_full = sem("work_full")
        work_drained = [sem("work_drained0"), sem("work_drained1")]
        hi_ready = sem("hi_ready")
        qk_high = sem("qk_high")
        k_twice = sem("k_twice")
        score_full = sem("score_full")
        smax_ready = sem("smax_ready")
        exp_ready = sem("exp_ready")
        rinv_ready = sem("rinv_ready")
        probs_ready = sem("probs_ready")
        turn_full = sem("turn_full")
        pT_ready = [sem("pT_ready0"), sem("pT_ready1")]
        ctx_full = sem("ctx_full")
        ctx_ready = sem("ctx_ready")
        resid_ready = sem("resid_ready")
        h2p_ready = sem("h2p_ready")
        tanh_ready = sem("tanh_ready")
        gate_ready = sem("gate_ready")
        th_ready = sem("th_ready")
        logits_full = sem("logits_full")
        logits_used = sem("logits_used")
        dstat_step = sem("dstat_step")
        rows_ready = sem("rows_ready")
        rlo_ready = sem("rlo_ready")
        r_spread = sem("r_spread")
        hu_ready = sem("hu_ready")
        relu_ready = sem("relu_ready")
        max_ready = sem("max_ready")
        edge_ready = sem("edge_ready")
        last_edge_ready = sem("last_edge_ready")
        agg_done = sem("agg_done")
        num_drained = sem("num_drained")
        den_drained = sem("den_drained")
        rden_ready = sem("rden_ready")
        pos_ready = sem("pos_ready")
        elu_exp = sem("elu_exp")
        diff_ready = sem("diff_ready")
        gated = sem("gated")
        out_ready = sem("out_ready")

        waits_passed = {e.engine: sem(f"waits_passed{i}")
                        for i, e in enumerate((nc.sync, nc.gpsimd, nc.vector, nc.tensor))}

        NCONST = 6

        def bank_of(g, *name):
            return work[place(g, *name)[0]]

        def mark_drained(ins, g, *name):
            ins.then_inc(work_drained[place(g, *name)[0]], 1)

        def drained(eng, g, *name):
            bank, before, _ = place(g, *name)
            eng.wait_ge(work_drained[bank], START + before + 1)

        def work_free(eng, g, *name):
            bank, before, _ = place(g, *name)
            eng.wait_ge(work_drained[bank], START + before)

        def prime(eng, *sems):
            for s in sems:
                eng.sem_inc(s, START)

        def settle(eng):
            eng.sem_inc(waits_passed[eng.engine], 1)

        def filled(eng, g, *name):
            eng.wait_ge(work_full, place(g, *name)[2] + 1)

        HI = 2 * TT + NPAIR
        STEPS = NG * TT

        block = ctx.enter_context(nc.Block())

        @block.sync
        def _(sp):
            def load_weights(*which):
                for n in which:
                    sp.dma_start(stage[n], w_dram[n].rearrange("(c p) n -> p c n", p=P)).then_inc(weight_in[n], 16)

            def load_x(b):
                sp.dma_start(x_in[:], x[b].rearrange("(t p) d -> p t d", p=P)).then_inc(x_loaded, 16)

            def load_adj(b):
                sp.dma_start(adj_u8[:], adj[b].rearrange("(t p) n -> p t n", p=P)).then_inc(adj_loaded, 16)

            def load_res(b):
                sp.dma_start(xres[:], x[b].rearrange("(t p) d -> p t d", p=P)).then_inc(res_loaded, 16)

            def store(b):
                for t in range(TT):
                    sp.wait_ge(out_ready, START + b * TT + t + 1)
                    settle(sp)
                    sp.dma_start(out[b, t * P:(t + 1) * P, :], xres[:, t]).then_inc(out_stored, 16)

            load_x(0)
            for dst, src in ((ident_f[:], ident), (pick_stage, pick_in), (bias_c[:], bc), (bias_f[:], bf),
                             (bias_h[:], hb), (wsd_f[:], wsd.rearrange("(c p) n -> p c n", p=P))):
                sp.dma_start(dst, src).then_inc(consts_in, 16)
            load_weights("wq", "wk", "wv")
            load_adj(0)
            load_weights("wf", "w1", "hw")
            load_res(0)
            with sp.Fori(0, B - 1) as b:
                sp.wait_ge(hi_ready, b * HI + TT)
                settle(sp)
                load_x(b + 1)
                sp.wait_ge(mask_ready, b + 1)
                settle(sp)
                load_adj(b + 1)
                store(b)
                sp.wait_ge(out_stored, START + (b + 1) * 16 * TT)
                settle(sp)
                load_res(b + 1)
            store(B - 1)
            sp.wait_ge(out_stored, START + B * 16 * TT)

        @block.gpsimd
        def _(pool):
            prime(pool, out_stored, out_ready, gated, last_edge_ready)
            nc.gpsimd.memset(mhalf[:], -0.5).then_inc(pool_setup, 1)
            nc.gpsimd.memset(uq_rows[:], 0.0).then_inc(pool_setup, 1)
            nc.gpsimd.memset(u_den[:], 0.0).then_inc(pool_setup, 1)
            pool.wait_ge(pool_setup, 3)

            def make_mask(g):
                pool.wait_ge(adj_loaded, 16 * g + 16)
                settle(pool)
                for t in range(TT):
                    ins = nc.gpsimd.tensor_scalar(mask[:, t], adj_u8[:, t], -NEG, NEG, ALU.mult, ALU.add)
                ins.then_inc(mask_ready, 1)

            def normalise(g, h):
                pool.wait_ge(rinv_ready, START + g * NH0 + h + 1)
                settle(pool)
                for t in range(TT):
                    pr = probs[h % 3][:, t]
                    nc.gpsimd.tensor_scalar(pr, pr, rinv[:, h, t:t + 1], 1.0,
                                            ALU.mult, ALU.mult).then_inc(probs_ready, 1)

            def root(g, k):
                for t in range(TT):
                    pool.wait_ge(var_ready, (2 * g + k) * TT + t + 1)
                    s = slice(t, t + 1)
                    nc.gpsimd.tensor_tensor(rstd[:, s], var[:, s], mhalf[:, s], ALU.pow).then_inc(rstd_ready, 1)

            def norm1(g):
                for t in range(TT):
                    pool.wait_ge(shift_ready, 2 * g * TT + t + 1)
                    settle(pool)
                    nc.gpsimd.tensor_scalar(x_in[:, t], x_in[:, t], rstd[:, t:t + 1], shift[:, t:t + 1],
                                            ALU.mult, ALU.add).then_inc(xn_ready, 1)

            def double_keys(g, p, before=None):
                n = g * NPAIR + p
                pool.wait_ge(qk_high, n * 2 + 2)
                if before is not None:
                    pool.wait_ge(*before)
                settle(pool)
                s = p % 2
                for i in range(2):
                    lo, o = i * DH0, (1 - i) * DH0
                    nc.gpsimd.tensor_scalar(kh[o:o + DH0, s, i], kh[lo:lo + DH0, s, i].bitcast(F32), 1.0, 1.0,
                                            ALU.mult, ALU.mult).then_inc(k_twice, 1)
                    pool.wait_ge(k_twice, n * 2 + i + 1)
                    settle(pool)

            def make_gate(b, t):
                pool.wait_ge(tanh_ready, b * TT + t + 1)
                settle(pool)
                nc.gpsimd.tensor_scalar(gate[:, t], gate[:, t], 0.5, 0.5, ALU.mult, ALU.add).then_inc(gate_ready, 1)

            def times_u(b, c):
                if c == 0:
                    drained(pool, b, "uq", 0)
                drained(pool, b, "tok", c)
                h = h_tok[:, c].rearrange("p (a e) -> p a e", a=NH1)
                nc.gpsimd.tensor_tensor(h, h, uqT[:, c, 0:NH1].unsqueeze(2).to_broadcast([P, NH1, DH1]),
                                        ALU.mult).then_inc(hu_ready, 1)

            def last_edge(b, n):
                pool.wait_ge(max_ready, b * STEPS + n + 1)
                if n >= 2:
                    pool.wait_ge(agg_done, b * STEPS + n - 1)
                nc.gpsimd.tensor_tensor(edge[:, (n * HG + HG - 1) % 8], t_ring[:, n % 2], adjT[:, n % TT],
                                        ALU.mult).then_inc(last_edge_ready, 1)

            def add_out(b, t):
                n = b * TT + t
                pool.wait_ge(diff_ready, START + n + 1)
                pool.wait_ge(out_ready, START + n)
                nc.gpsimd.tensor_tensor(fin_g[:], fin_q[:, t], gate[:, t], ALU.mult).then_inc(gated, 1)
                pool.wait_ge(gated, START + n + 1)
                nc.gpsimd.tensor_tensor(xres[:, t], fin_g[:], xres[:, t], ALU.add).then_inc(out_ready, 1)

            def graph(b, more):
                normalise(b, 1)
                normalise(b, 2)
                double_keys(b, 2, (probs_ready, (b * NH0 + 3) * TT))
                normalise(b, 3)
                normalise(b, 4)
                normalise(b, 5)
                pool.wait_ge(res_loaded, 16 * b + 16)
                for t in range(TT):
                    ins = nc.gpsimd.tensor_tensor(xres[:, t], xres[:, t], bias_f[:], ALU.add)
                ins.then_inc(xb_ready, 1)
                root(b, 1)
                for t in range(TT):
                    pool.wait_ge(hn_ready, b * TT + t + 1)
                    nc.gpsimd.tensor_tensor(xres[:, t], xres[:, t], hn[:, t], ALU.add).then_inc(resid_ready, 1)
                filled(pool, b, "norm2", TT - 1)
                pool.wait_ge(resid_ready, (b + 1) * TT)
                settle(pool)
                for t in range(TT):
                    nc.gpsimd.tensor_scalar(hn[:, t], hn[:, t], 1.0, 1.0, ALU.add, ALU.mult).then_inc(h2p_ready, 1)
                if more:
                    root(b + 1, 0)
                    norm1(b + 1)
                for n in range(STEPS):
                    if n < TT:
                        times_u(b, n)
                    last_edge(b, n)
                    if n in (1, 2, 3):
                        for t in ((0, 1), (2,), (3,))[n - 1]:
                            make_gate(b, t)
                    if more and n == 4:
                        filled(pool, b, "adj", TT - 1)
                        make_mask(b + 1)
                    if more and n in (8, 10):
                        double_keys(b + 1, n // 2 - 4, (last_edge_ready, START + b * STEPS + n + 1))
                add_out(b, 0)
                if more:
                    normalise(b + 1, 0)
                add_out(b, 1)
                add_out(b, 2)
                add_out(b, 3)

            root(0, 0)
            norm1(0)
            make_mask(0)
            double_keys(0, 0, (mask_ready, 1))
            double_keys(0, 1)
            normalise(0, 0)
            with pool.Fori(0, B - 1) as b:
                graph(b, True)
            graph(B - 1, False)

        @block.scalar
        def _(act):
            prime(act, num_drained, pT_ready[1])

            def weight_high(n):
                act.wait_ge(weight_in[n], 16)
                nc.scalar.activation(w_hi[n][:], stage[n], ACT.Copy,
                                     scale=-SCALE if n == "wq" else 1.0).then_inc(split_hi, 1)

            def norm2(b, t):
                act.wait_ge(shift_ready, (2 * b + 1) * TT + t + 1)
                nc.scalar.activation(hn[:, t], xres[:, t], ACT.Relu,
                                     bias=shift[:, t:t + 1], scale=rstd[:, t:t + 1]).then_inc(hn_ready, 1)

            def turned_high(g, name, t):
                filled(act, g, name, t)
                nc.scalar.activation(hT_hi[:, :, t * P:(t + 1) * P],
                                     bank_of(g, name, t)[:, 0:D].rearrange("p (c n) -> p c n", c=FC),
                                     ACT.Relu).then_inc(hi_ready, 1)

            def qk_hi(g, p, name):
                s, col = p % 2, "qk".index(name) * NPAIR + p
                filled(act, g, name, p)
                ps = bank_of(g, name, p)
                for i in range(2):
                    lo, hi = i * DH0, (i + 1) * DH0
                    ins = nc.scalar.activation((qs if name == "q" else kh)[lo:hi, s, i], ps[lo:hi], ACT.Identity,
                                               bias=bias_c[lo:hi, col:col + 1])
                ins.then_inc(qk_high, 1)

            def value(g, t):
                filled(act, g, "v", t)
                mark_drained(nc.scalar.activation(v_tok[:, t], bank_of(g, "v", t)[:, 0:D], ACT.Copy), g, "v", t)

            def exps(g, h, tiles=range(TT)):
                for t in tiles:
                    i = h * TT + t
                    act.wait_ge(smax_ready, START + g * NH0 * TT + i + 1)
                    if t == 0 and h >= 3:
                        act.wait_ge(turn_full, (g * NH0 + h - 2) * TT)
                    if t == 0 and h == 2:
                        act.wait_ge(diff_ready, START + g * TT)
                    if t == 0:
                        act.wait_ge(rinv_ready, START + g * NH0)
                    nc.scalar.activation(probs[h % 3][:, t], sm[:, i % 2], ACT.Exp, scale=-1.0,
                                         bias=nmax[:, h, t:t + 1],
                                         accum_out=rsum[:, h, t:t + 1]).then_inc(exp_ready, 1)

            def pT_copy(b, h, c):
                if h == 1 and c == 1:
                    act.wait_ge(gated, START + b * TT)
                if h in (2, 3) and c == 1:
                    act.wait_ge(ctx_full, b * NPAIR + 1)
                act.wait_ge(turn_full, (b * NH0 + h) * TT + c + 1)
                nc.scalar.activation((pT_early if h < 4 else pT_late)[h % 2][:, c], turn[1][:],
                                     ACT.Copy).then_inc(pT_ready[1], 1)

            def ctx_high(b, p):
                act.wait_ge(ctx_full, b * NPAIR + p + 1)
                nc.scalar.activation(ctx_hi[:, p], acc[p % 2][:], ACT.Identity,
                                     bias=bias_c[:, 2 * NPAIR + p:2 * NPAIR + p + 1]).then_inc(hi_ready, 1)

            def adj_copy(b, c):
                filled(act, b, "adj", c)
                act.wait_ge(edge_ready, START + b * STEPS * (HG - 1))
                act.wait_ge(last_edge_ready, START + b * STEPS)
                mark_drained(nc.scalar.activation(adjT[:, c], bank_of(b, "adj", c)[:, 0:N // 2].bitcast(BF16),
                                                  ACT.Relu, scale=-1.0, bias=1.0), b, "adj", c)

            def elu(b, t):
                act.wait_ge(pos_ready, b * TT + t + 1)
                nc.scalar.activation(fin_f[:, t % 2], fin_f[:, t % 2], ACT.Exp).then_inc(elu_exp, 1)

            def tanh_gate(b, t):
                drained(act, b, "gate", t)
                nc.scalar.activation(gate[:, t], gate[:, t], ACT.Tanh, scale=0.5).then_inc(tanh_ready, 1)

            def last_maxima(b, n):
                g, c = n // TT, n % TT
                h = g * HG + HG - 1
                if c == 0:
                    act.wait_ge(r_spread, b * NH1 + h + 1)
                act.wait_ge(last_edge_ready, START + b * STEPS + max(n - 1, 0))
                nc.scalar.activation(t_ring[:, n % 2], rbank[HG - 1][:], ACT.Relu, bias=nqT[:, c, h:h + 1]
                                     ).then_inc(relu_ready, 1)
                act.wait_ge(relu_ready, b * STEPS + n + 1)
                nc.scalar.activation(t_ring[:, n % 2], t_ring[:, n % 2], ACT.Identity,
                                     bias=uqT[:, c, DROW + h:DROW + h + 1]).then_inc(max_ready, 1)

            def sums_copy(b, g):
                act.wait_ge(agg_done, b * STEPS + (g + 1) * TT)
                nc.scalar.activation(numT[:, g], acc[0][:], ACT.Copy).then_inc(num_drained, 1)

            def graph(b, more):
                def turn_and_exps(h):
                    pT_copy(b, h, 1)
                    exps(b, h + 2, (0, 1))
                    pT_copy(b, h, 3)
                    exps(b, h + 2, (2, 3))

                turn_and_exps(0)
                qk_hi(b, 2, "q")
                turn_and_exps(1)
                qk_hi(b, 2, "k")
                adj_copy(b, 0)
                ctx_high(b, 0)
                adj_copy(b, 1)
                turn_and_exps(2)
                turn_and_exps(3)
                for h in (4, 5):
                    pT_copy(b, h, 1)
                    pT_copy(b, h, 3)
                    ctx_high(b, h - 3)
                norm2(b, 0)
                for t in range(TT):
                    if t + 1 < TT:
                        norm2(b, t + 1)
                    turned_high(b, "norm2", t)
                adj_copy(b, 2)
                adj_copy(b, 3)
                tanh_gate(b, 0)
                for c in range(FC):
                    filled(act, b, "feat", c)
                    ps = bank_of(b, "feat", c)
                    nc.scalar.activation(th[:, c], ps[:], ACT.Tanh).then_inc(th_ready, 1)
                    mark_drained(nc.scalar.activation(feat[:, c], ps[:], ACT.Identity,
                                                      bias=bias_c[:, 3 * NPAIR:3 * NPAIR + 1]), b, "feat", c)
                for t in range(TT):
                    filled(act, b, "tok", t)
                    mark_drained(nc.scalar.activation(h_tok[:, t], bank_of(b, "tok", t)[:, 0:D], ACT.Copy),
                                 b, "tok", t)
                act.wait_ge(dstat_step, b * 5 + 5)
                nc.scalar.activation(uq_rows[0:NH1], dd_rows[DROW:ROWS], ACT.Exp)
                nc.scalar.activation(uq_rows[DROW:ROWS], dd_rows[DROW:ROWS], ACT.Exp,
                                     scale=LEAKY - 1.0).then_inc(rows_ready, 1)
                act.wait_ge(logits_used, b + 1)
                nc.scalar.activation(r_full, x_rows, ACT.Exp, scale=1.0 - LEAKY)
                nc.scalar.activation(r_rows[0:NH1], x_rows, ACT.Exp, scale=1.0 - LEAKY).then_inc(rows_ready, 1)
                tanh_gate(b, 1)
                drained(act, b, "uq", 0)
                for n in range(STEPS):
                    last_maxima(b, n)
                    if n == 0:
                        tanh_gate(b, 2)
                    if n == 1:
                        tanh_gate(b, 3)
                    if more and n in (1, 2, 3):
                        for t in ((0, 1), (2,), (3,))[n - 1]:
                            turned_high(b + 1, "norm1", t)
                    if more and n in (5, 6, 7, 8):
                        qk_hi(b + 1, (n - 5) // 2, "kq"[n % 2])
                    if more and n == 9:
                        value(b + 1, 0)
                    if n % TT == 0 and n > 0:
                        sums_copy(b, n // TT - 1)
                if more:
                    act.wait_ge(agg_done, b * STEPS + STEPS - 1)
                    exps(b + 1, 0, (0,))
                sums_copy(b, NG - 1)
                if more:
                    exps(b + 1, 0, (1, 2))
                for t in range(TT):
                    elu(b, t)
                    if more and t == TT - 1:
                        value(b + 1, 1)
                    if more:
                        i = t + 3
                        exps(b + 1, i // TT, (i % TT,))
                if more:
                    value(b + 1, 2)
                    value(b + 1, 3)
                    exps(b + 1, 1, (3,))

            weight_high("wq")
            weight_high("wk")
            for t in range(TT):
                turned_high(0, "norm1", t)
            weight_high("wv")
            act.wait_ge(consts_ready, 1)
            for p in range(2):
                qk_hi(0, p, "q")
                qk_hi(0, p, "k")
            for t in range(TT):
                value(0, t)
            exps(0, 0)
            exps(0, 1)
            for n in ("wf", "w1", "hw"):
                weight_high(n)
            act.wait_ge(split, len(names))
            with act.Fori(0, B - 1) as b:
                graph(b, True)
            graph(B - 1, False)

        @block.vector
        def _(dve):
            prime(dve, diff_ready, smax_ready, edge_ready, rinv_ready, pT_ready[0], *work_drained)
            nc.vector.memset(r_rows[:].bitcast(F32), 0.0)
            nc.vector.memset(kl[:].bitcast(F32), 0.0)

            def weight_low(n):
                i = names.index(n)
                dve.wait_ge(split_hi, i + 1)
                nc.vector.scalar_tensor_tensor(out=w_lo[n][:], in0=stage[n], scalar=-SCALE if n == "wq" else 1.0,
                                               in1=w_hi[n][:].bitcast(F32), op0=ALU.mult,
                                               op1=ALU.subtract).then_inc(split, 1)

            def tile_stats(g, k, t):
                nc.vector.bn_stats(stats[:, t], (xres if k else x_in)[:, t]).then_inc(stat_ready, 1)

            def mean(g, k, t):
                dve.wait_ge(stat_ready, (2 * g + k) * TT + t + 1)
                settle(dve)
                nc.vector.bn_aggr(mv[:, t], stats[:, t]).then_inc(mean_ready, 1)

            def variance(g, k, t):
                dve.wait_ge(mean_ready, (2 * g + k) * TT + t + 1)
                nc.vector.tensor_scalar(var[:, t:t + 1], mv[:, t, 1:2], EPS, None, ALU.add).then_inc(var_ready, 1)

            def shifts(g, k, t):
                dve.wait_ge(rstd_ready, (2 * g + k) * TT + t + 1)
                nc.vector.scalar_tensor_tensor(out=shift[:, t:t + 1], in0=mv[:, t, 0:1], scalar=-1.0,
                                               in1=rstd[:, t:t + 1], op0=ALU.mult, op1=ALU.mult
                                               ).then_inc(shift_ready, 1)

            def turned_low(g, k, name, t):
                dve.wait_ge(hi_ready, g * HI + k * (TT + NPAIR) + t + 1)
                s = slice(t * P, (t + 1) * P)
                mark_drained(nc.vector.scalar_tensor_tensor(
                    out=hT_lo[:, :, s], in0=bank_of(g, name, t)[:, 0:D].rearrange("p (c n) -> p c n", c=FC),
                    scalar=0.0, in1=hT_hi[:, :, s].bitcast(F32), op0=ALU.max, op1=ALU.subtract), g, name, t)

            def qk_low(g, p, name):
                s, w = p % 2, "qk".index(name)
                col = w * NPAIR + p
                dve.wait_ge(qk_high, (g * NPAIR + p) * 2 + w + 1)
                ps = bank_of(g, name, p)
                for i in range(2):
                    lo, hi = i * DH0, (i + 1) * DH0
                    o = (1 - i) * DH0
                    dst = qs[o:o + DH0, s, i] if w == 0 else kl[lo:hi, s, i]
                    ins = nc.vector.scalar_tensor_tensor(out=dst, in0=ps[lo:hi], scalar=bias_c[lo:hi, col:col + 1],
                                                         in1=(qs, kh)[w][lo:hi, s, i].bitcast(F32),
                                                         op0=ALU.add, op1=ALU.subtract)
                mark_drained(ins, g, name, p)

            def maxima(g, h, tiles=range(TT)):
                for t in tiles:
                    i = h * TT + t
                    dve.wait_ge(score_full, g * NH0 * TT + i + 1)
                    if i >= 2:
                        dve.wait_ge(exp_ready, g * NH0 * TT + i - 1)
                    settle(dve)
                    nc.vector.tensor_tensor_reduce(sm[:, i % 2], score[i % 2][:], mask[:, t], 1.0, 3.0e38,
                                                   ALU.add, ALU.min, nmax[:, h, t:t + 1]).then_inc(smax_ready, 1)

            def inverse(g, h):
                dve.wait_ge(exp_ready, (g * NH0 + h + 1) * TT)
                nc.vector.reciprocal(rinv[:, h], rsum[:, h]).then_inc(rinv_ready, 1)

            def pT_copy(b, h, c):
                if h == 1 and c == 0:
                    dve.wait_ge(gated, START + b * TT)
                if h in (2, 3) and c == 0:
                    dve.wait_ge(ctx_full, b * NPAIR + 1)
                dve.wait_ge(turn_full, (b * NH0 + h) * TT + c + 1)
                nc.vector.tensor_copy((pT_early if h < 4 else pT_late)[h % 2][:, c],
                                      turn[0][:]).then_inc(pT_ready[0], 1)

            def ctx_low(b, p):
                dve.wait_ge(hi_ready, b * HI + TT + p + 1)
                nc.vector.scalar_tensor_tensor(out=ctx_lo[:, p], in0=acc[p % 2][:],
                                               scalar=bias_c[:, 2 * NPAIR + p:2 * NPAIR + p + 1],
                                               in1=ctx_hi[:, p].bitcast(F32),
                                               op0=ALU.add, op1=ALU.subtract).then_inc(ctx_ready, 1)

            def residual(b, t):
                filled(dve, b, "out", t)
                mark_drained(nc.vector.tensor_tensor(xres[:, t], bank_of(b, "out", t)[:, 0:D], xres[:, t], ALU.add),
                             b, "out", t)

            def gate_sum(b, t):
                filled(dve, b, "gate", t)
                mark_drained(nc.vector.tensor_tensor(gate[:, t], bank_of(b, "gate", t)[:, 0:D], bias_h[:], ALU.add),
                             b, "gate", t)

            def edges(b, n):
                g, c = n // TT, n % TT
                for j in range(HG - 1):
                    if c == 0:
                        dve.wait_ge(r_spread, b * NH1 + g * HG + j + 1)
                    if j == 0 and n >= 2:
                        dve.wait_ge(agg_done, b * STEPS + n - 1)
                    q = DROW + g * HG + j
                    nc.vector.scalar_tensor_tensor(out=edge[:, (n * HG + j) % 8], in0=rbank[j][:],
                                                   scalar=uqT[:, c, q:q + 1], in1=adjT[:, c],
                                                   op0=ALU.max, op1=ALU.mult).then_inc(edge_ready, 1)

            def inverse_den(b, t):
                filled(dve, b, "fin", t)
                nc.vector.reciprocal(rden[:, t % 2], bank_of(b, "fin", t)[:, D:N].rearrange("p (j s) -> p s j", j=HG)
                                     [:, 0:NG]).then_inc(rden_ready, 1)

            def divide(b, t):
                dve.wait_ge(rden_ready, b * TT + t + 1)
                mark_drained(nc.vector.tensor_tensor(
                    fin_f[:, t % 2].rearrange("p (a e) -> p a e", a=NH1),
                    bank_of(b, "fin", t)[:, 0:D].rearrange("p (a e) -> p a e", a=NH1),
                    rden[:, t % 2].rearrange("p g j -> p (g j)").unsqueeze(2).to_broadcast([P, NH1, DH1]),
                    ALU.mult), b, "fin", t)

            def positive(b, t):
                drained(dve, b, "fin", t)
                dve.wait_ge(gated, START + b * TT)
                nc.vector.scalar_tensor_tensor(out=fin_q[:, t], in0=fin_f[:, t % 2], scalar=0.0, in1=hn[:, t],
                                               op0=ALU.max, op1=ALU.subtract).then_inc(pos_ready, 1)

            def difference(b, t):
                dve.wait_ge(elu_exp, b * TT + t + 1)
                nc.vector.scalar_tensor_tensor(out=fin_q[:, t], in0=fin_f[:, t % 2], scalar=1.0,
                                               in1=fin_q[:, t], op0=ALU.min, op1=ALU.add).then_inc(diff_ready, 1)

            def graph(b, more):
                def turn_and_maxima(h, after_copy=None, between=lambda: None):
                    pT_copy(b, h, 0)
                    if after_copy is not None:
                        inverse(b, after_copy)
                    maxima(b, h + 2, (0, 1))
                    between()
                    pT_copy(b, h, 2)
                    maxima(b, h + 2, (2, 3))

                turn_and_maxima(0, after_copy=1)
                turn_and_maxima(1, after_copy=2, between=lambda: qk_low(b, 2, "q"))
                qk_low(b, 2, "k")
                inverse(b, 3)
                ctx_low(b, 0)
                turn_and_maxima(2)
                turn_and_maxima(3, after_copy=4)
                pT_copy(b, 4, 0)
                inverse(b, 5)
                pT_copy(b, 4, 2)
                pT_copy(b, 5, 0)
                ctx_low(b, 1)
                pT_copy(b, 5, 2)
                ctx_low(b, 2)
                dve.wait_ge(xb_ready, b + 1)
                residual(b, 0)
                residual(b, 1)
                for t in (0, 1):
                    drained(dve, b, "out", t)
                    tile_stats(b, 1, t)
                for t in (0, 1):
                    mean(b, 1, t)
                for t in (0, 1):
                    variance(b, 1, t)
                residual(b, 2)
                drained(dve, b, "out", 2)
                tile_stats(b, 1, 2)
                shifts(b, 1, 0)
                mean(b, 1, 2)
                variance(b, 1, 2)
                residual(b, 3)
                shifts(b, 1, 1)
                drained(dve, b, "out", 3)
                tile_stats(b, 1, 3)
                turned_low(b, 1, "norm2", 0)
                mean(b, 1, 3)
                variance(b, 1, 3)
                shifts(b, 1, 2)
                turned_low(b, 1, "norm2", 1)
                shifts(b, 1, 3)
                gate_sum(b, 0)
                turned_low(b, 1, "norm2", 2)
                turned_low(b, 1, "norm2", 3)
                if more:
                    dve.wait_ge(x_loaded, 16 * b + 32)
                    for step in (tile_stats, mean, variance, shifts):
                        for t in range(TT):
                            step(b + 1, 0, t)
                s0 = b * 5
                dve.wait_ge(logits_full, b + 1)
                rows = acc[1]
                nc.vector.tensor_reduce(dstat[DROW:ROWS, 0:1], rows[DROW:ROWS], AX_X, ALU.max).then_inc(dstat_step, 1)
                nc.vector.tensor_reduce(dstat[DROW:ROWS, 1:2], rows[DROW:ROWS], AX_X, ALU.min).then_inc(dstat_step, 1)
                dve.wait_ge(dstat_step, s0 + 2)
                nc.vector.tensor_tensor(dstat[DROW:ROWS, 1:2], dstat[DROW:ROWS, 0:1], dstat[DROW:ROWS, 1:2],
                                        ALU.subtract).then_inc(dstat_step, 1)
                dve.wait_ge(dstat_step, s0 + 3)
                nc.vector.tensor_copy(dstat[0:NH1, 0:2], dstat[DROW:ROWS, 0:2]).then_inc(dstat_step, 1)
                nc.vector.tensor_scalar(dd_rows[DROW:ROWS], rows[DROW:ROWS], dstat[DROW:ROWS, 0:1], None,
                                        ALU.subtract).then_inc(dstat_step, 1)
                dve.wait_ge(dstat_step, s0 + 5)
                nc.vector.tensor_scalar(x_rows, rows[0:NH1], dstat[0:NH1, 0:1], dstat[0:NH1, 1:2],
                                        ALU.add, ALU.min).then_inc(logits_used, 1)
                gate_sum(b, 1)
                filled(dve, b, "uq", 0)
                uq_ps = bank_of(b, "uq", 0)[:, 0:TT * ROWS].rearrange("p (c r) -> p c r", c=TT)
                nc.vector.tensor_scalar(nqT[:], uq_ps[:, :, DROW:ROWS], -1.0, None, ALU.mult)
                for g in range(NG):
                    nc.vector.tensor_copy(u_den[:, :, g, :, g], uq_ps[:, :, g * HG:(g + 1) * HG])
                mark_drained(nc.vector.tensor_copy(uqT[:], uq_ps), b, "uq", 0)
                dve.wait_ge(rows_ready, 2 * b + 2)
                nc.vector.tensor_tensor(r_rows[DROW:ROWS], r_full, r_rows[0:NH1].bitcast(F32),
                                        ALU.subtract).then_inc(rlo_ready, 1)
                gate_sum(b, 2)
                drained(dve, b, "uq", 0)
                for n in range(STEPS):
                    edges(b, n)
                    if n == 0:
                        gate_sum(b, 3)
                    if not more:
                        continue
                    if n in (1, 2, 3):
                        for t in ((0,), (1,), (2, 3))[n - 1]:
                            turned_low(b + 1, 0, "norm1", t)
                    if n in (5, 6, 7, 8):
                        qk_low(b + 1, (n - 5) // 2, "kq"[n % 2])
                if more:
                    dve.wait_ge(mask_ready, b + 2)
                    maxima(b + 1, 0, (0, 1))
                dve.wait_ge(agg_done, (b + 1) * STEPS)
                nc.vector.tensor_copy(denT, acc[1][:]).then_inc(den_drained, 1)
                if more:
                    maxima(b + 1, 0, (2,))
                dve.wait_ge(gate_ready, (b + 1) * TT)
                dve.wait_ge(h2p_ready, (b + 1) * TT)
                for t in range(TT + 1):
                    if t < TT:
                        inverse_den(b, t)
                    if more and t > 0:
                        maxima(b + 1, (t + 2) // TT, ((t + 2) % TT,))
                    if t < TT:
                        divide(b, t)
                    if more and t == 2:
                        inverse(b + 1, 0)
                    if t > 0:
                        difference(b, t - 1)
                    if t < TT:
                        positive(b, t)
                if more:
                    maxima(b + 1, 1, (3,))

            dve.wait_ge(x_loaded, 16)
            for step in (tile_stats, mean, variance, shifts):
                for t in range(TT):
                    step(0, 0, t)
            dve.wait_ge(consts_in, 16 * NCONST)
            nc.vector.tensor_copy(ident_b[:], ident_f[:])
            nc.vector.tensor_copy(pick[:], pick_stage)
            nc.vector.tensor_scalar(bias_c[:, 0:NPAIR], bias_c[:, 0:NPAIR], -SCALE, None,
                                    ALU.mult).then_inc(consts_ready, 1)
            dve.wait_ge(consts_ready, 1)
            weight_low("wq")
            weight_low("wk")
            for t in range(TT):
                turned_low(0, 0, "norm1", t)
            weight_low("wv")
            for p in range(2):
                qk_low(0, p, "q")
                qk_low(0, p, "k")
            dve.wait_ge(mask_ready, 1)
            maxima(0, 0)
            maxima(0, 1, [0])
            inverse(0, 0)
            maxima(0, 1, range(1, TT))
            for n in ("wf", "w1", "hw"):
                weight_low(n)
            dve.wait_ge(split, len(names))
            with dve.Fori(0, B - 1) as b:
                graph(b, True)
            graph(B - 1, False)

        @block.tensor
        def _(pe):
            pe.wait_ge(consts_in, 16 * NCONST)

            def three(ps, l_hi, l_lo, r_hi, r_lo, chunks=range(FC)):
                for c in chunks:
                    for i, (l, r) in enumerate(((l_hi, r_hi), (l_hi, r_lo), (l_lo, r_hi))):
                        ins = nc.tensor.matmul(ps, l(c), r(c), start=(c == 0 and i == 0),
                                               stop=(c == FC - 1 and i == 2))
                return ins

            def cols(t, lo):
                return lambda c: t[:, c, lo:lo + P]

            def whole(t):
                return lambda c: t[:, c, :]

            def turn_norm(g, k, name, t):
                work_free(pe, g, name, t)
                pe.wait_ge((xn_ready, hn_ready)[k], g * TT + t + 1)
                for c in range(FC):
                    ins = nc.tensor.transpose(bank_of(g, name, t)[:, c * P:(c + 1) * P],
                                              (x_in, hn)[k][:, t, c * P:(c + 1) * P], ident_f[:])
                ins.then_inc(work_full, 1)

            def by_feature(g, name, w, c):
                work_free(pe, g, name, c)
                three(bank_of(g, name, c)[:], cols(w_hi[w], c * P), cols(w_lo[w], c * P), whole(hT_hi),
                      whole(hT_lo)).then_inc(work_full, 1)

            def by_node(g, name, l_hi, l_lo, w, t, chunks=range(FC)):
                if 0 in chunks:
                    work_free(pe, g, name, t)
                ins = three(bank_of(g, name, t)[:, 0:D], cols(l_hi, t * P), cols(l_lo, t * P), whole(w_hi[w]),
                            whole(w_lo[w]), chunks)
                if FC - 1 in chunks:
                    ins.then_inc(work_full, 1)

            def hT_ready(g, name):
                drained(pe, g, name, TT - 2)
                drained(pe, g, name, TT - 1)

            def query_key(g, p, name):
                by_feature(g, name, "w" + name, p)

            def values(g, t):
                by_node(g, "v", hT_hi, hT_lo, "wv", t)

            def scores(g, h, tiles=range(TT)):
                s, i = (h // 2) % 2, h % 2
                for t in tiles:
                    n = h * TT + t
                    if i == 0 and t == 0:
                        drained(pe, g, "q", h // 2)
                        drained(pe, g, "k", h // 2)
                        pe.wait_ge(k_twice, (g * NPAIR + h // 2 + 1) * 2)
                    if n < 2:
                        if not isinstance(g, int):
                            pe.wait_ge(edge_ready, START + g * STEPS * (HG - 1) - 2 + n)
                    else:
                        pe.wait_ge(smax_ready, START + g * NH0 * TT + n - 1)
                    q = qs[:, s, i, t * P:(t + 1) * P]
                    nc.tensor.matmul(score[n % 2][:], q, kh[:, s, i], start=True, stop=False)
                    nc.tensor.matmul(score[n % 2][:], q, kl[:, s, i], start=False, stop=True).then_inc(score_full, 1)

            def turn_probs(b, h, c):
                for t in range(TT):
                    if c == 0:
                        pe.wait_ge(probs_ready, b * NH0 * TT + h * TT + t + 1)
                    if t == 0:
                        pe.wait_ge(pT_ready[c % 2], START + b * NH0 * 2 + (h * TT + c) // 2)
                    ins = nc.tensor.transpose(turn[c % 2][:, t * P:(t + 1) * P], probs[h % 3][:, t, c * P:(c + 1) * P],
                                              ident_f[:])
                ins.then_inc(turn_full, 1)

            def context(b, p, c):
                if p == 0 and c == 0:
                    pe.wait_ge(num_drained, START + b * NG)
                    drained(pe, b, "v", TT - 2)
                    drained(pe, b, "v", TT - 1)
                if p == 2 and c == 0:
                    pe.wait_ge(ctx_ready, b * NPAIR + 1)
                pe.wait_ge(pT_ready[c % 2], START + b * NH0 * 2 + (2 * p + 1) * 2 + c // 2 + 1)
                for i in range(2):
                    f = (2 * p + i) * DH0
                    ins = nc.tensor.matmul(acc[p % 2][i * DH0:(i + 1) * DH0], v_tok[:, c, f:f + DH0],
                                           (pT_late if p == 2 else pT_early)[i][:, c],
                                           start=(c == 0), stop=(c == TT - 1))
                if c == TT - 1:
                    ins.then_inc(ctx_full, 1)

            def turn_adj(b, c):
                work_free(pe, b, "adj", c)
                for t in range(TT):
                    ins = nc.tensor.transpose(bank_of(b, "adj", c)[:, t * P // 2:(t + 1) * P // 2].bitcast(BF16),
                                              mask[:, t, c * P:(c + 1) * P], ident_b[:])
                ins.then_inc(work_full, 1)

            def gate_product(b, t):
                by_node(b, "gate", hT_hi, hT_lo, "hw", t)

            def logits(b, c):
                pe.wait_ge(th_ready, b * FC + c + 1)
                ins = nc.tensor.matmul(acc[1][0:ROWS], wsd_f[:, c], th[:, c], start=(c == 0), stop=(c == FC - 1))
                if c == FC - 1:
                    ins.then_inc(logits_full, 1)

            def turn_feat(b, t):
                work_free(pe, b, "tok", t)
                for c in range(FC):
                    ins = nc.tensor.transpose(bank_of(b, "tok", t)[:, c * P:(c + 1) * P],
                                              feat[:, c, t * P:(t + 1) * P], ident_f[:])
                ins.then_inc(work_full, 1)

            def spread(b, g, j):
                if g > 0:
                    if j < HG - 1:
                        pe.wait_ge(edge_ready, START + b * STEPS * (HG - 1) + (g * TT - 1) * (HG - 1) + j + 1)
                    else:
                        pe.wait_ge(relu_ready, b * STEPS + g * TT)
                h = g * HG + j
                nc.tensor.matmul(rbank[j][:], pick[:, h:h + 1].to_broadcast([P, P]), r_rows[:], start=True,
                                 stop=True).then_inc(r_spread, 1)

            def aggregate(b, n):
                g, c = n // TT, n % TT
                pe.wait_ge(edge_ready, START + b * STEPS * (HG - 1) + (n + 1) * (HG - 1))
                pe.wait_ge(last_edge_ready, START + b * STEPS + n + 1)
                if g == 0:
                    pe.wait_ge(hu_ready, b * TT + c + 1)
                if c == 0 and g > 0:
                    pe.wait_ge(num_drained, START + b * NG + g)
                for j in range(HG):
                    f = (g * HG + j) * DH1
                    nc.tensor.matmul(acc[0][j * DH1:(j + 1) * DH1], h_tok[:, c, f:f + DH1],
                                     edge[:, (n * HG + j) % 8], start=(c == 0), stop=(c == TT - 1),
                                     skip_group_check=True)
                for j in range(HG):
                    ins = nc.tensor.matmul(acc[1][j * DH1:(j + 1) * DH1], u_den[:, c, g, j],
                                           edge[:, (n * HG + j) % 8], start=(n == 0),
                                           stop=(n == STEPS - 1), skip_group_check=True)
                ins.then_inc(agg_done, 1)

            def turn_sums(b, t):
                if t == 0:
                    pe.wait_ge(num_drained, START + (b + 1) * NG)
                    pe.wait_ge(den_drained, b + 1)
                work_free(pe, b, "fin", t)
                ps = bank_of(b, "fin", t)
                for g in range(NG):
                    nc.tensor.transpose(ps[:, g * P:(g + 1) * P], numT[:, g, t * P:(t + 1) * P], ident_f[:])
                nc.tensor.transpose(ps[:, D:N], denT[:, t * P:(t + 1) * P], ident_f[:]).then_inc(work_full, 1)

            def graph(b, more):
                def turn_and_scores(h):
                    for c in range(TT):
                        turn_probs(b, h, c)
                        scores(b, h + 2, (c,))

                turn_and_scores(0)
                query_key(b, 2, "q")
                turn_and_scores(1)
                query_key(b, 2, "k")
                turn_adj(b, 0)
                for c in range(TT):
                    context(b, 0, c)
                turn_adj(b, 1)
                turn_and_scores(2)
                turn_and_scores(3)
                for c in range(TT):
                    turn_probs(b, 4, c)
                    context(b, 1, c)
                turn_probs(b, 5, 0)
                for c in range(TT):
                    if c + 1 < TT:
                        turn_probs(b, 5, c + 1)
                    context(b, 2, c)
                pe.wait_ge(split, len(names))
                for chunks in ((0, 1), (2,)):
                    if chunks == (2,):
                        pe.wait_ge(ctx_ready, (b + 1) * NPAIR)
                    else:
                        pe.wait_ge(ctx_ready, b * NPAIR + 2)
                    for t in (0, 1):
                        by_node(b, "out", ctx_hi, ctx_lo, "wf", t, chunks)
                for t in (2, 3):
                    by_node(b, "out", ctx_hi, ctx_lo, "wf", t)
                turn_norm(b, 1, "norm2", 0)
                turn_norm(b, 1, "norm2", 1)
                drained(pe, b, "norm2", 0)
                gate_product(b, 0)
                turn_norm(b, 1, "norm2", 2)
                turn_norm(b, 1, "norm2", 3)
                turn_adj(b, 2)
                turn_adj(b, 3)
                hT_ready(b, "norm2")
                by_feature(b, "feat", "w1", 0)
                by_feature(b, "feat", "w1", 1)
                logits(b, 0)
                by_feature(b, "feat", "w1", 2)
                logits(b, 1)
                logits(b, 2)
                drained(pe, b, "feat", 1)
                drained(pe, b, "feat", 2)
                for t in range(TT):
                    turn_feat(b, t)
                gate_product(b, 1)
                pe.wait_ge(rows_ready, 2 * b + 1)
                work_free(pe, b, "uq", 0)
                settle(pe)
                for c in range(TT):
                    ins = nc.tensor.transpose(bank_of(b, "uq", 0)[:, c * ROWS:(c + 1) * ROWS],
                                              uq_rows[:, c * P:(c + 1) * P], ident_f[0:ROWS, 0:ROWS])
                ins.then_inc(work_full, 1)
                gate_product(b, 2)
                pe.wait_ge(rlo_ready, b + 1)
                for j in range(HG):
                    spread(b, 0, j)
                gate_product(b, 3)
                if more:
                    turn_norm(b + 1, 0, "norm1", 0)
                for n in range(STEPS):
                    if more and n == STEPS - 1:
                        scores(b + 1, 0, (0, 1))
                    aggregate(b, n)
                    if n % TT == TT - 2 and n < STEPS - 2:
                        for j in range(HG):
                            spread(b, n // TT + 1, j)
                    if not more:
                        continue
                    if n in (0, 1, 2):
                        for t in ((1,), (2,), (3,))[n]:
                            turn_norm(b + 1, 0, "norm1", t)
                    if n == 3:
                        hT_ready(b + 1, "norm1")
                    if n in (3, 4, 5, 6):
                        query_key(b + 1, (n - 3) // 2, "kq"[n % 2])
                    if n == 7:
                        values(b + 1, 0)
                if more:
                    scores(b + 1, 0, (2,))
                for t in range(TT):
                    turn_sums(b, t)
                    if more:
                        scores(b + 1, (t + 3) // TT, ((t + 3) % TT,))
                if more:
                    values(b + 1, 1)
                    values(b + 1, 2)
                    values(b + 1, 3)
                    scores(b + 1, 1, (3,))

            for t in range(TT):
                turn_norm(0, 0, "norm1", t)
            hT_ready(0, "norm1")
            pe.wait_ge(split, 2)
            for p in range(2):
                query_key(0, p, "q")
                query_key(0, p, "k")
            pe.wait_ge(split, 3)
            for t in range(TT):
                values(0, t)
            scores(0, 0)
            scores(0, 1)
            pe.wait_ge(consts_ready, 1)
            with pe.Fori(0, B - 1) as b:
                graph(b, True)
            graph(B - 1, False)


def host_layout(a):
    def rep(v):
        return np.ascontiguousarray(np.broadcast_to(v, (P, D)))

    wsd = np.zeros((D, ROWS), np.float32)
    for h in range(NH1):
        wsd[h * DH1:(h + 1) * DH1, h] = a["L1_gnn_w_src"][h, :, 0]
        wsd[h * DH1:(h + 1) * DH1, DROW + h] = a["L1_gnn_w_dst"][h, :, 0]
    pick = np.zeros((P, NH1), np.float32)
    for h in range(NH1):
        pick[h, h] = 1.0
        pick[DROW + h, h] = 1.0
    return {
        "x": a["x"], "adj": a["adj"],
        "wq": a["L0_gnn_Wq"], "wk": a["L0_gnn_Wk"], "wv": a["L0_gnn_Wv"], "wf": a["L0_gnn_Wf"],
        "w1": a["L1_gnn_W"].transpose(1, 0, 2).reshape(D, D), "hw": a["L1_gnn_H_w"].T,
        "bc": np.concatenate([a["L0_gnn_b" + n].reshape(FC, P).T for n in "qkv"]
                             + [np.tile(a["L1_gnn_b"], HG)[:, None]], axis=1),
        "bf": rep(a["L0_gnn_bf"]),
        "hb": rep(a["L1_gnn_H_b"]),
        "wsd": wsd, "ident": np.eye(P, dtype=np.float32),
        "pick_in": pick,
    }


def kernel(**inputs):
    import concourse.bacc as bacc
    from concourse.bass_utils import run_bass_kernel_spmd

    arrays = host_layout({k: np.asarray(v) for k, v in inputs.items()})
    nc = bacc.Bacc("TRN2", target_bir_lowering=False, num_devices=1)
    feed, aps = {}, {}
    for name, v in arrays.items():
        v = np.ascontiguousarray(v)
        feed["in_" + name] = v
        aps[name] = nc.dram_tensor("in_" + name, v.shape, mybir.dt.from_np(v.dtype), kind="ExternalInput").ap()
    out = nc.dram_tensor("out_x", (B, N, D), F32, kind="ExternalOutput").ap()
    build(nc, **aps, out=out)
    r = run_bass_kernel_spmd(nc, [feed], core_ids=[0])
    return r.results[0]["out_x"]
```
